# Optimizing a Trainium2 kernel written in Bass

```python
import numpy as np
import jax
import jax.numpy as jnp

def _softmax(x, axis=-1):
    return jax.nn.softmax(x, axis=axis)

def _gelu(x):
    return jax.nn.gelu(x, approximate=True)

def _silu(x):
    return jax.nn.silu(x)

def _sigmoid(x):
    return jax.nn.sigmoid(x)

def _layernorm(x, axis=-1, eps=1e-05):
    m = jnp.mean(x, axis=axis, keepdims=True)
    v = jnp.var(x, axis=axis, keepdims=True)
    return (x - m) / jnp.sqrt(v + eps)

def _scatter_add(tgt, idx, src, axis=0):
    return tgt.at[idx].add(src)

def _segment_sum(src, seg, n):
    return jax.ops.segment_sum(src, seg, n)
kernel_name = 'mk_seq_preln_d1_jaxref_r4_71f852'

def setup_inputs(seed: int=0):
    np.random.seed(seed)
    _w = jnp.asarray

    def _L0_attn_setup():
        import jax, jax.numpy as jnp
        import numpy as np
        D_MODEL = 256
        N_HEADS = 16
        D_K = D_MODEL // N_HEADS
        SEQ = 1024
        BATCH = 2
        LOCAL_WINDOW = 128
        SCALE = 1.0 / float(np.sqrt(D_K))
        INIT = 1.0 / float(np.sqrt(D_MODEL))

        def _local_mask(seq_len: int) -> jnp.ndarray:
            i = jnp.arange(seq_len)[:, None]
            j = jnp.arange(seq_len)[None, :]
            return (j <= i) & (j >= i - LOCAL_WINDOW)
        key = jax.random.key(seed)
        ks = jax.random.split(key, 9)
        mk = lambda k: jax.random.normal(k, (D_MODEL, D_MODEL), dtype=jnp.float32) * INIT
        return {'x': jax.random.normal(ks[0], (BATCH, SEQ, D_MODEL), dtype=jnp.float32), 'Wq': mk(ks[1]), 'bq': jnp.zeros((D_MODEL,), jnp.float32), 'Wk': mk(ks[2]), 'bk': jnp.zeros((D_MODEL,), jnp.float32), 'Wv': mk(ks[3]), 'bv': jnp.zeros((D_MODEL,), jnp.float32), 'Wo': mk(ks[4]), 'bo': jnp.zeros((D_MODEL,), jnp.float32)}
    _L0_attn_in = _L0_attn_setup()

    def _L0_ffn_setup():
        import jax, jax.numpy as jnp
        import numpy as np
        key = jax.random.key(seed)
        kx, kw = jax.random.split(key)
        x = jax.random.normal(kx, (32, 1024, 256), dtype=jnp.float32)
        weight = jax.random.normal(kw, (256, 256), dtype=jnp.float32) * 0.01
        return {'x': x, 'weight': weight}
    _L0_ffn_in = _L0_ffn_setup()
    _d = {'L0_attn_x': _L0_attn_in['x'], 'L0_attn_Wq': _L0_attn_in['Wq'], 'L0_attn_bq': _L0_attn_in['bq'], 'L0_attn_Wk': _L0_attn_in['Wk'], 'L0_attn_bk': _L0_attn_in['bk'], 'L0_attn_Wv': _L0_attn_in['Wv'], 'L0_attn_bv': _L0_attn_in['bv'], 'L0_attn_Wo': _L0_attn_in['Wo'], 'L0_attn_bo': _L0_attn_in['bo'], 'L0_ffn_weight': _L0_ffn_in['weight']}
    _x0 = _d['L0_attn_x']
    _d['L0_attn_x'] = jax.random.normal(jax.random.fold_in(jax.random.key(seed), 1), (8, 1024, 256), dtype=_x0.dtype)
    del _x0
    return _d

def reference(L0_attn_x, L0_attn_Wq, L0_attn_bq, L0_attn_Wk, L0_attn_bk, L0_attn_Wv, L0_attn_bv, L0_attn_Wo, L0_attn_bo, L0_ffn_weight):

    def _L0_attn_ref(x, Wq, bq, Wk, bk, Wv, bv, Wo, bo):
        import jax, jax.numpy as jnp
        import numpy as np
        D_MODEL = 256
        N_HEADS = 16
        D_K = D_MODEL // N_HEADS
        SEQ = 1024
        BATCH = 2
        LOCAL_WINDOW = 128
        SCALE = 1.0 / float(np.sqrt(D_K))
        INIT = 1.0 / float(np.sqrt(D_MODEL))

        def _local_mask(seq_len: int) -> jnp.ndarray:
            i = jnp.arange(seq_len)[:, None]
            j = jnp.arange(seq_len)[None, :]
            return (j <= i) & (j >= i - LOCAL_WINDOW)
        B, S, _ = x.shape
        q = (x @ Wq.T + bq).reshape(B, S, N_HEADS, D_K)
        k = (x @ Wk.T + bk).reshape(B, S, N_HEADS, D_K)
        v = (x @ Wv.T + bv).reshape(B, S, N_HEADS, D_K)
        scores = jnp.einsum('bqhd,bkhd->bhqk', q, k) * SCALE
        mask = _local_mask(S)[None, None]
        scores = jnp.where(mask, scores, jnp.float32(-10000.0))
        attn = jax.nn.softmax(scores, axis=-1) + jnp.float32(1e-09)
        ctx = jnp.einsum('bhqk,bkhd->bqhd', attn, v).reshape(B, S, D_MODEL)
        return ctx @ Wo.T + bo

    def _L0_ffn_ref(x, weight):
        import jax, jax.numpy as jnp
        import numpy as np
        b_weight = jnp.sign(weight)
        return jnp.einsum('bsi,oi->bso', x, b_weight)
    x = L0_attn_x
    x = x + _L0_attn_ref(_layernorm(x, axis=-1), L0_attn_Wq, L0_attn_bq, L0_attn_Wk, L0_attn_bk, L0_attn_Wv, L0_attn_bv, L0_attn_Wo, L0_attn_bo)
    x = x + _L0_ffn_ref(_layernorm(x, axis=-1), L0_ffn_weight)
    return x

_drawn_inputs = setup_inputs


def setup_inputs(seed=0):
    import zlib

    import numpy as np

    out = dict(_drawn_inputs(seed))
    spreads = {'L0_attn_bq': (0.0, 0.539),
     'L0_attn_bk': (0.0, 0.8),
     'L0_attn_bv': (0.0, 0.1),
     'L0_attn_bo': (0.0, 0.1)}
    factors = {}
    for name, (base, spread) in spreads.items():
        noise = np.random.default_rng([zlib.crc32(name.encode()), seed]).standard_normal(out[name].shape)
        drawn = base * np.exp(spread * noise) if base else spread * noise
        out[name] = jnp.asarray(drawn.astype(out[name].dtype))
    for name, factor in factors.items():
        out[name] = (out[name] * factor).astype(out[name].dtype)
    return out
```

```python
from contextlib import ExitStack

import concourse.bass as bass
from concourse import mybir

F32 = mybir.dt.float32
F32R = mybir.dt.float32r
BF16 = mybir.dt.bfloat16
ACT = mybir.ActivationFunctionType
ALU = mybir.AluOpType
AX = mybir.AxisListType

P = 128
H = 16
DK = 16
D = H * DK
C = D // P
HB = H // C
TILES = 8
PAIRS = TILES // 2
ROWS = TILES * P
QB = 32
WIN = QB + P
SCALE = 0.25
EPS = 1e-5
SPREAD = 1e-9
MASKED = -1e30
SUMS = 3 * DK + 1
SC_FILLS = 8
MX_FILLS = [(rg, heads) for heads in ((0, 1, 2), (3, 4, 5), (6, 7)) for rg in range(C)]
MXF = len(MX_FILLS)


def build(nc, x, wq_t, wk_t, wv_t, wo_t, wf_t, bq_c, bk_c, bv_c, bo_r, out):
    BATCHES = x.shape[0]
    LAST = BATCHES - 1
    NT = BATCHES * TILES
    x_pair = x.rearrange("b (g t p) d -> b g p t d", t=2, p=P)
    x_tile = x.rearrange("b (t p) d -> b t p d", p=P)
    y_tile = out.rearrange("b (t p) d -> b t p d", p=P)

    with ExitStack() as ctx:
        def sb(name, shape, dt=F32):
            return ctx.enter_context(nc.sbuf_tensor(name, shape, dt))

        def bank(name):
            return ctx.enter_context(nc.psum_tensor(name, [P, 512], F32))

        def sem(name):
            return ctx.enter_context(nc.semaphore(name))

        w_hi = {n: sb(f"wh_{n}", [P, C, D], F32R) for n in "qkvo"}
        w_lo = {n: sb(f"wl_{n}", [P, C, D], F32R) for n in "qkvo"}
        w_sign = sb("w_sign", [P, C, D], F32R)
        bq = sb("bq", [P, C])
        bk = sb("bk", [P, C])
        bv = sb("bv", [P, C])
        bvs = sb("bvs", [P, C])
        bo = sb("bo", [P, D])
        ident = sb("ident", [P, P])
        ident16 = sb("ident16", [P, P], BF16)
        ones = sb("ones", [P, P])
        window = sb("window", [P, 3, WIN], BF16)
        window0 = sb("window0", [P, 3, WIN], BF16)
        half = sb("half", [P, 2])
        xs = sb("xs", [P, 2, 2, D])
        st1 = sb("st1", [P, 2, 6])
        mv1 = sb("mv1", [P, 2, 2])
        ve1 = sb("ve1", [P, 2])
        rs1 = sb("rs1", [P, 2])
        xn = sb("xn", [P, 2, D])
        xt_hi = sb("xt_hi", [P, C, 2 * P], F32R)
        xt_lo = sb("xt_lo", [P, C, 2 * P], F32R)
        q_hi = sb("q_hi", [P, C, 2 * P], F32R)
        q_lo = sb("q_lo", [P, C, 2 * P], F32R)
        q_16 = sb("q_16", [P, C, 2 * P], BF16)
        k_hi = sb("k_hi", [P, C, 2 * P], F32R)
        k_lo = sb("k_lo", [P, C, 2 * P], F32R)
        k_16 = sb("k_16", [P, C, 2 * P], BF16)
        q_stack = sb("q_stack", [P, HB, ROWS], F32R)
        k_stack = sb("k_stack", [P, HB, ROWS], F32R)
        q_max = sb("q_max", [P, HB, ROWS], BF16)
        k_max = sb("k_max", [P, HB, P + ROWS], BF16)
        v_ones = sb("v_ones", [P, TILES, H, 2 * DK])
        vsum = sb("vsum", [P, D])
        nmax = sb("nmax", [P, 2, H])
        nmax_t = sb("nmax_t", [H, 2, P], F32R)
        prob = sb("prob", [P, 2, H, 2 * P])
        raw = prob[:, :, :, :].rearrange("p r h q -> p (r h q)").rearrange("p (n c d) -> p n c d", c=C, d=D)
        w_raw = {n: raw[:, i] for i, n in enumerate("qkvof")}
        w_pos, w_neg = raw[:, 5], raw[:, 6]
        u = sb("u", [P, 2, 512])
        rden = sb("rden", [P, H])
        cx = sb("cx", [P, H, DK])
        ct_hi = sb("ct_hi", [P, C, P], F32R)
        ct_lo = sb("ct_lo", [P, C, P], F32R)
        cb_hi = sb("cb_hi", [P, C, P], F32R)
        cb_lo = sb("cb_lo", [P, C, P], F32R)
        brow = sb("brow", [P, D])
        cb = brow[:, :].rearrange("p (c q) -> p c q", c=C)
        xr = sb("xr", [P, 2, D])
        x2 = sb("x2", [P, 2, D])
        st2 = sb("st2", [P, 6])
        mv2 = sb("mv2", [P, 2])
        ve2 = sb("ve2", [P, 1])
        rs2 = sb("rs2", [P, 1])
        xn2 = sb("xn2", [P, D])
        t2_hi = sb("t2_hi", [P, C, P], F32R)
        t2_lo = sb("t2_lo", [P, C, P], F32R)

        sc_bank = [bank("sc0"), bank("sc1")]
        mx_bank = bank("mx")
        pv_bank = [bank("pv0"), bank("pv1")]
        ga = bank("ga")
        gb = bank("gb")
        gc = bank("gc")

        w_loaded = {n: sem(f"w_loaded_{n}") for n in "qkvof"}
        b_loaded = sem("b_loaded")
        x_loaded = [sem("x_loaded0"), sem("x_loaded1")]
        q_stacked = [sem("q_stacked0"), sem("q_stacked1")]
        k_stacked = [sem("k_stacked0"), sem("k_stacked1")]
        nmax_stacked = [sem("nmax_stacked0"), sem("nmax_stacked1")]
        xr_loaded = [sem("xr_loaded0"), sem("xr_loaded1")]
        y_stored = [sem("y_stored0"), sem("y_stored1")]
        settled = {e: sem(f"settled_{n}") for n, e in (("sp", nc.sync.engine), ("pool", nc.gpsimd.engine), ("dve", nc.vector.engine))}
        consts_done = sem("consts_done")
        memset_done = sem("memset_done")
        pool_setup = sem("pool_setup")
        w_hi_done = sem("w_hi_done")
        w_lo_done = sem("w_lo_done")
        w_sign_done = sem("w_sign_done")
        bvs_done = sem("bvs_done")
        bn1_done, mv1_done, ve1_done, rs1_done, xn_done = map(sem, ("bn1_done", "mv1_done", "ve1_done", "rs1_done", "xn_done"))
        t1_filled, xt_hi_done, xt_lo_done = map(sem, ("t1_filled", "xt_hi_done", "xt_lo_done"))
        q_filled, q_hi_done, q_16_done, q_lo_done = map(sem, ("q_filled", "q_hi_done", "q_16_done", "q_lo_done"))
        k_filled, k_hi_done, k_16_done, k_lo_done = map(sem, ("k_filled", "k_hi_done", "k_16_done", "k_lo_done"))
        v_filled, v_done, vsum_step = map(sem, ("v_filled", "v_done", "vsum_step"))
        cb_filled, cb_step, br_filled, brow_done = map(sem, ("cb_filled", "cb_step", "br_filled", "brow_done"))
        sc_filled = sem("sc_filled")
        exp_done = sem("exp_done")
        prob_masked = sem("prob_masked")
        mx_filled = sem("mx_filled")
        mx_done = sem("mx_done")
        nm_filled, nm_done = map(sem, ("nm_filled", "nm_done"))
        pv_filled, u_done = map(sem, ("pv_filled", "u_done"))
        ut_filled, rden_done, cx_done = map(sem, ("ut_filled", "rden_done", "cx_done"))
        ct_filled, ct_hi_done, ct_lo_done = map(sem, ("ct_filled", "ct_hi_done", "ct_lo_done"))
        op_filled, xb_done, x2_done, bn2_done, mv2_done = map(sem, ("op_filled", "xb_done", "x2_done", "bn2_done", "mv2_done"))
        ve2_done, rs2_done, xn2_done = map(sem, ("ve2_done", "rs2_done", "xn2_done"))
        t2_filled, t2_hi_done, t2_lo_done = map(sem, ("t2_filled", "t2_hi_done", "t2_lo_done"))
        ff_filled, y_done = map(sem, ("ff_filled", "y_done"))

        def wait(eng, s, n):
            if not isinstance(n, int) or n > 0:
                eng.wait_ge(s, n)

        def settle(eng, n):
            if not isinstance(n, int):
                eng.sem_inc(settled[eng.engine], 1)

        def halves(t):
            return t % 2, t // 2

        def parts(b, t):
            def tile(shift):
                bb, tt = b + (t + shift) // TILES, (t + shift) % TILES
                if isinstance(b, int) and not 0 <= bb <= LAST:
                    return None
                return bb, tt

            def pair(shift):
                n = t + shift
                if n % 2:
                    return None
                bb, pp = b + n // TILES, n // 2 % PAIRS
                if isinstance(b, int) and not 0 <= bb <= LAST:
                    return None
                return bb, pp

            if isinstance(b, int) and b > LAST:
                now = None
            else:
                now = (b, t)
            return now, {"nm": tile(2), "mx": tile(3), "pv": tile(-1), "xr": tile(-2), "op": tile(-3), "ff": tile(-4),
                         "tqv": pair(5), "k": pair(4), "ln": pair(6), "load": pair(7)}

        def run(eng, slot):
            for t in range(TILES):
                slot(0, t)
            with eng.Fori(1, LAST) as b:
                for t in range(TILES):
                    slot(b, t)
            for t in range(TILES):
                slot(LAST, t)
            for t in range(4):
                slot(BATCHES, t)

        block = ctx.enter_context(nc.Block())

        @block.sync
        def _(sp):
            def load_x(b, p):
                i, n = halves(p)
                wait(sp, xn_done, PAIRS * b + p - 1)
                settle(sp, b)
                sp.dma_start(xs[:, i], x_pair[b, p]).then_inc(x_loaded[i], 16)

            def stack(b, p, hi, lo, b16, stack_, max_, shift, order, hi_done, lo_done, b16_done, stacked):
                i, _ = halves(p)
                cols = slice(2 * P * p, 2 * P * (p + 1))
                g = PAIRS * b + p
                wait(sp, sc_filled, SC_FILLS * (TILES * (b - 1) + 2 * p + 2))
                settle(sp, b)
                sp.wait_ge(hi_done, g + 1)
                sp.wait_ge(lo_done, g + 1)
                sp.wait_ge(b16_done, g + 1)
                settle(sp, g)
                for c in range(C):
                    for r, part in enumerate(order):
                        src = (hi, lo)[part]
                        at = 64 * c + DK * r
                        sp.dma_start(stack_[at:at + DK, :, cols].bitcast(F32),
                                     src[:, c, :].bitcast(F32)).then_inc(stacked[i], 16)
                    sp.dma_start(max_[64 * c:64 * c + DK, :, shift + 2 * P * p:shift + 2 * P * (p + 1)],
                                 b16[:, c, :]).then_inc(stacked[i], 16)

            def stack_q(b, p):
                stack(b, p, q_hi, q_lo, q_16, q_stack, q_max, 0, (0, 0, 1), q_hi_done, q_lo_done, q_16_done, q_stacked)

            def stack_k(b, p):
                stack(b, p, k_hi, k_lo, k_16, k_stack, k_max, P, (0, 1, 0), k_hi_done, k_lo_done, k_16_done, k_stacked)

            def stack_nmax(b, t):
                i, _ = halves(t)
                sp.wait_ge(nm_done, TILES * b + t + 1)
                settle(sp, b)
                for c in range(C):
                    at = 64 * c + 3 * DK
                    sp.dma_start(q_stack[at:at + 1, :, P * t:P * (t + 1)].bitcast(F32),
                                 nmax_t[HB * c:HB * (c + 1), i, :].bitcast(F32)).then_inc(nmax_stacked[i], 16)

            def load_xr(b, t):
                i, _ = halves(t)
                wait(sp, x2_done, TILES * b + t - 1)
                settle(sp, b)
                sp.dma_start(xr[:, i], x_tile[b, t]).then_inc(xr_loaded[i], 16)

            def slot(b, t):
                now, part = parts(b, t)
                if part["nm"]:
                    stack_nmax(*part["nm"])
                if part["load"]:
                    load_x(*part["load"])
                if part["tqv"]:
                    stack_q(*part["tqv"])
                if part["k"]:
                    stack_k(*part["k"])
                if part["xr"]:
                    load_xr(*part["xr"])
                if part["ff"]:
                    bb, tt = part["ff"]
                    i, _ = halves(tt)
                    sp.wait_ge(y_done, TILES * bb + tt + 1)
                    settle(sp, bb)
                    sp.dma_start(y_tile[bb, tt], x2[:, i]).then_inc(y_stored[i], 16)

            load_x(0, 0)
            load_x(0, 1)
            sp.wait_ge(memset_done, 4)
            load_x(0, 2)
            stack_q(0, 0)
            stack_k(0, 0)
            load_x(0, 3)
            stack_q(0, 1)
            stack_k(0, 1)
            stack_nmax(0, 0)
            stack_q(0, 2)
            stack_nmax(0, 1)
            run(sp, slot)
            for i in range(2):
                sp.wait_ge(y_stored[i], 16 * (NT // 2))

        @block.gpsimd
        def _(pool):
            g = nc.gpsimd
            g.memset(half[:, :], -0.5)
            g.memset(ident[:, :], 0.0)
            g.memset(window[:, :, :], 0.0)
            g.memset(window0[:, :, :], 0.0).then_inc(pool_setup, 1)
            pool.wait_ge(pool_setup, 1)
            g.affine_select(out=ident[:, :], in_=ident[:, :], compare_op=ALU.not_equal, fill=1.0, base=0,
                            pattern=[[1, P]], channel_multiplier=-1).then_inc(pool_setup, 1)
            n = 2
            for mask in (window, window0):
                for blk in range(P // QB):
                    m = mask[QB * blk:QB * (blk + 1), :, :]
                    for base, cm, step in ((0, -1, 1), (P, 1, -1)):
                        pool.wait_ge(pool_setup, n)
                        g.affine_select(out=m, in_=m, compare_op=ALU.is_ge, fill=MASKED, base=base,
                                        pattern=[[0, 3], [step, WIN]], channel_multiplier=cm).then_inc(pool_setup, 1)
                        n += 1
            for blk in range(P // QB):
                m = window0[QB * blk:QB * (blk + 1), :, :]
                pool.wait_ge(pool_setup, n)
                g.affine_select(out=m, in_=m, compare_op=ALU.is_ge, fill=MASKED, base=QB * blk - P,
                                pattern=[[0, 3], [1, WIN]], channel_multiplier=0).then_inc(pool_setup, 1)
                n += 1
            pool.wait_ge(pool_setup, n)
            g.tensor_copy(ident16[:, :], ident[:, :]).then_inc(consts_done, 1)

            def rsqrt1(b, p):
                n = PAIRS * b + p
                pool.wait_ge(mv1_done, n + 1)
                settle(pool, n)
                g.tensor_scalar(ve1[:, :], mv1[:, :, 1], EPS, None, ALU.add).then_inc(ve1_done, 1)
                pool.wait_ge(ve1_done, n + 1)
                g.tensor_tensor(rs1[:, :], ve1[:, :], half[:, :], ALU.pow).then_inc(rs1_done, 1)

            def sum_v(b, p):
                pool.wait_ge(v_done, PAIRS * b + p + 1)
                for j in range(2):
                    n = TILES * b + 2 * p + j
                    v = v_ones[:, 2 * p + j, :, 0:DK]
                    s = vsum[:, :].rearrange("p (h d) -> p h d", h=H)
                    if p == 0 and j == 0:
                        wait(pool, cb_filled, b)
                        settle(pool, b)
                        g.tensor_copy(s, v).then_inc(vsum_step, 1)
                    else:
                        pool.wait_ge(vsum_step, n)
                        g.tensor_tensor(s, s, v, ALU.add).then_inc(vsum_step, 1)

            def mask_probs(b, t, r):
                n = TILES * b + t
                pool.wait_ge(exp_done, SC_FILLS * n + 4 * (r + 1))
                settle(pool, n)
                pr = prob[:, t % 2, HB * r:HB * (r + 1), :]
                if t < TILES - 1:
                    nxt = pr[:, :, P:2 * P]
                    g.affine_select(out=nxt, in_=nxt, compare_op=ALU.is_ge, fill=0.0, base=0,
                                    pattern=[[0, HB], [-1, P]], channel_multiplier=1)
                own = pr[:, :, 0:P]
                g.affine_select(out=own, in_=own, compare_op=ALU.is_ge, fill=0.0, base=0,
                                pattern=[[0, HB], [1, P]], channel_multiplier=-1).then_inc(prob_masked, 1)

            def add_biases(b, t):
                i, n = halves(t)
                pool.wait_ge(brow_done, b + 1)
                pool.wait_ge(xr_loaded[i], 16 * (TILES // 2 * b + n + 1))
                g.tensor_tensor(xr[:, i], xr[:, i], brow[:, :], ALU.add).then_inc(xb_done, 1)

            def rsqrt2(b, t):
                n = TILES * b + t
                pool.wait_ge(mv2_done, n + 1)
                settle(pool, n)
                g.tensor_scalar(ve2[:, :], mv2[:, 1:2], EPS, None, ALU.add).then_inc(ve2_done, 1)
                pool.wait_ge(ve2_done, n + 1)
                g.tensor_tensor(rs2[:, :], ve2[:, :], half[:, 0:1], ALU.pow).then_inc(rs2_done, 1)

            def slot(b, t):
                now, part = parts(b, t)
                if part["pv"]:
                    mask_probs(*part["pv"], 1)
                if part["ln"]:
                    rsqrt1(*part["ln"])
                if part["k"]:
                    sum_v(*part["k"])
                if part["op"]:
                    add_biases(*part["op"])
                if now:
                    mask_probs(*now, 0)
                if part["op"]:
                    rsqrt2(*part["op"])

            rsqrt1(0, 0)
            rsqrt1(0, 1)
            sum_v(0, 0)
            rsqrt1(0, 2)
            sum_v(0, 1)
            run(pool, slot)

        @block.scalar
        def _(act):
            a = nc.scalar
            for n, w in zip("qkvof", (wq_t, wk_t, wv_t, wo_t, wf_t)):
                act.dma_start(w_raw[n], w.rearrange("(c p) n -> p c n", p=P)).then_inc(w_loaded[n], 16)
                if n == "q":
                    for dst, src in ((bq, bq_c), (bk, bk_c), (bv, bv_c), (bo, bo_r)):
                        act.dma_start(dst[:, :], src).then_inc(b_loaded, 16)
            for n in "qkvo":
                act.wait_ge(w_loaded[n], 16)
                a.activation(w_hi[n][:, :, :], w_raw[n], ACT.Copy).then_inc(w_hi_done, 1)
            act.wait_ge(b_loaded, 64)

            def xt_part(b, p):
                n = PAIRS * b + p
                act.wait_ge(t1_filled, n + 1)
                wait(act, k_filled, n)
                a.activation(xt_hi[:, :, :], gc[:, :].rearrange("p (c q) -> p c q", c=C), ACT.Copy).then_inc(xt_hi_done, 1)

            def qk_part(b, p, filled, hi, b16, bias, hi_done, b16_done, stacked):
                i, _ = halves(p)
                n = PAIRS * b + p
                act.wait_ge(filled, n + 1)
                if not isinstance(n, int) or n > 0:
                    j = (p - 1) % 2
                    bb, pp = (b, p - 1) if p else (b - 1, PAIRS - 1)
                    act.wait_ge(stacked[j], 128 * (PAIRS // 2 * bb + pp // 2 + 1))
                for c in range(C):
                    last = a.activation(hi[:, c, :], gc[:, 2 * P * c:2 * P * (c + 1)], ACT.Identity, bias=bias[:, c:c + 1])
                last.then_inc(hi_done, 1)
                act.wait_ge(hi_done, n + 1)
                a.activation(b16[:, :, :], hi[:, :, :].bitcast(F32), ACT.Copy).then_inc(b16_done, 1)

            def v_part(b, p):
                n = PAIRS * b + p
                act.wait_ge(v_filled, n + 1)
                wait(act, pv_filled, TILES * (b - 1) + 2 * p + 2)
                wait(act, vsum_step, TILES * b)
                a.activation(v_ones[:, 2 * p:2 * p + 2, :, 0:DK],
                             gc[:, :].rearrange("p (t h d) -> p t h d", t=2, h=H), ACT.Copy).then_inc(v_done, 1)

            def exp(b, t, f):
                n = TILES * b + t
                q = 2 * P if t < TILES - 1 else P
                act.wait_ge(sc_filled, SC_FILLS * n + f + 1)
                if f == 0:
                    wait(act, pv_filled, n - 1)
                    if isinstance(n, int) and n == 0:
                        act.wait_ge(w_lo_done, 4)
                        act.wait_ge(w_sign_done, 2)
                a.activation(prob[:, t % 2, 2 * f:2 * f + 2, 0:q],
                             sc_bank[f % 2][:, :].rearrange("p (h q) -> p h q", h=2)[:, :, 0:q],
                             ACT.Exp, scale=SCALE).then_inc(exp_done, 1)

            def nmax_part(b, t):
                i, m = halves(t)
                n = TILES * b + t
                act.wait_ge(nm_filled, n + 1)
                wait(act, nmax_stacked[i], 32 * (TILES // 2 * b + m))
                a.activation(nmax_t[:, i, :], gb[0:H, 0:P], ACT.Copy).then_inc(nm_done, 1)

            def slot(b, t):
                now, part = parts(b, t)
                if now:
                    exp(b, t, 0)
                if part["nm"]:
                    nmax_part(*part["nm"])
                if now:
                    exp(b, t, 1)
                if part["tqv"]:
                    xt_part(*part["tqv"])
                if now:
                    exp(b, t, 2)
                if part["ff"]:
                    bb, tt = part["ff"]
                    n = TILES * bb + tt
                    act.wait_ge(t2_filled, n + 1)
                    wait(act, ff_filled, n)
                    a.activation(t2_hi[:, :, :], gb[:, 0:D].rearrange("p (c q) -> p c q", c=C), ACT.Copy).then_inc(t2_hi_done, 1)
                if now:
                    exp(b, t, 3)
                if part["tqv"]:
                    qk_part(*part["tqv"], q_filled, q_hi, q_16, bq, q_hi_done, q_16_done, q_stacked)
                if part["k"]:
                    qk_part(*part["k"], k_filled, k_hi, k_16, bk, k_hi_done, k_16_done, k_stacked)
                if now:
                    exp(b, t, 4)
                if part["op"]:
                    bb, tt = part["op"]
                    n = TILES * bb + tt
                    act.wait_ge(ct_filled, n + 1)
                    wait(act, op_filled, n)
                    a.activation(ct_hi[:, :, :], gb[:, 0:D].rearrange("p (c q) -> p c q", c=C), ACT.Copy).then_inc(ct_hi_done, 1)
                if now:
                    exp(b, t, 5)
                    exp(b, t, 6)
                if part["pv"]:
                    bb, tt = part["pv"]
                    n = TILES * bb + tt
                    act.wait_ge(pv_filled, n + 1)
                    wait(act, ut_filled, n - 1)
                    a.activation(u[:, tt % 2, :], pv_bank[tt % 2][:, :], ACT.Copy).then_inc(u_done, 1)
                if now:
                    exp(b, t, 7)
                if part["tqv"]:
                    v_part(*part["tqv"])

            def project(b, p):
                xt_part(b, p)
                qk_part(b, p, q_filled, q_hi, q_16, bq, q_hi_done, q_16_done, q_stacked)
                v_part(b, p)

            act.wait_ge(memset_done, 5)
            project(0, 0)
            qk_part(0, 0, k_filled, k_hi, k_16, bk, k_hi_done, k_16_done, k_stacked)
            project(0, 1)
            qk_part(0, 1, k_filled, k_hi, k_16, bk, k_hi_done, k_16_done, k_stacked)
            nmax_part(0, 0)
            project(0, 2)
            nmax_part(0, 1)
            run(act, slot)

        @block.vector
        def _(dve):
            v = nc.vector
            v.memset(q_stack[:, :, :].bitcast(F32), 0.0).then_inc(memset_done, 1)
            v.memset(k_stack[:, :, :].bitcast(F32), 1.0).then_inc(memset_done, 1)
            v.memset(k_max[:, :, :], 0.0).then_inc(memset_done, 1)
            v.memset(q_max[:, :, :], 0.0).then_inc(memset_done, 1)
            v.memset(v_ones[:, :, :, :], 1.0).then_inc(memset_done, 1)
            v.memset(ones[:, :], 1.0)

            def stats1(b, p):
                i, m = halves(p)
                n = PAIRS * b + p
                dve.wait_ge(x_loaded[i], 16 * (PAIRS // 2 * b + m + 1))
                wait(dve, mv1_done, n)
                for j in range(2):
                    last = v.bn_stats(st1[:, j], xs[:, i, j])
                last.then_inc(bn1_done, 1)
                dve.wait_ge(bn1_done, n + 1)
                wait(dve, xn_done, n)
                settle(dve, n)
                for j in range(2):
                    last = v.bn_aggr(mv1[:, j], st1[:, j])
                last.then_inc(mv1_done, 1)

            def norm1(b, p):
                i, _ = halves(p)
                n = PAIRS * b + p
                dve.wait_ge(rs1_done, n + 1)
                wait(dve, t1_filled, n)
                for j in range(2):
                    last = v.tensor_scalar(xn[:, j], xs[:, i, j], mv1[:, j, 0:1], rs1[:, j:j + 1],
                                           ALU.subtract, ALU.mult)
                last.then_inc(xn_done, 1)

            def norm2(b, t):
                i, _ = halves(t)
                n = TILES * b + t
                dve.wait_ge(rs2_done, n + 1)
                wait(dve, t2_filled, n)
                v.tensor_scalar(xn2[:, :], x2[:, i], mv2[:, 0:1], rs2[:, :],
                                ALU.subtract, ALU.mult).then_inc(xn2_done, 1)

            def xt_part(b, p):
                n = PAIRS * b + p
                dve.wait_ge(xt_hi_done, n + 1)
                v.tensor_tensor(xt_lo[:, :, :], gc[:, :].rearrange("p (c q) -> p c q", c=C),
                                xt_hi[:, :, :].bitcast(F32), ALU.subtract).then_inc(xt_lo_done, 1)

            def qk_part(b, p, hi, lo, bias, hi_done, lo_done):
                dve.wait_ge(hi_done, PAIRS * b + p + 1)
                for c in range(C):
                    last = v.scalar_tensor_tensor(lo[:, c, :], gc[:, 2 * P * c:2 * P * (c + 1)], bias[:, c:c + 1],
                                                  hi[:, c, :].bitcast(F32), ALU.add, ALU.subtract)
                last.then_inc(lo_done, 1)

            def row_max(b, t, f):
                rg, heads = MX_FILLS[f]
                n = MXF * (TILES * b + t) + f
                dve.wait_ge(mx_filled, n + 1)
                if f == 0:
                    wait(dve, nm_filled, TILES * b + t - 1)
                h0 = HB * rg + heads[0]
                v.tensor_reduce(nmax[:, t % 2, h0:h0 + len(heads)],
                                mx_bank[:, 0:WIN * len(heads)].rearrange("p (h k) -> p h k", k=WIN),
                                AX.X, ALU.max, negate=True).then_inc(mx_done, 1)

            def normalise(b, t):
                n = TILES * b + t
                dve.wait_ge(ut_filled, n + 1)
                ut = ga[:, :].rearrange("p (h e) -> p h e", h=H)
                v.reciprocal(rden[:, :], ut[:, :, DK]).then_inc(rden_done, 1)
                dve.wait_ge(rden_done, n + 1)
                wait(dve, ct_filled, n)
                v.tensor_tensor(cx[:, :, :], ut[:, :, 0:DK], rden[:, :].unsqueeze(2).broadcast_to([P, H, DK]),
                                ALU.mult).then_inc(cx_done, 1)

            def spread_bias(b):
                dve.wait_ge(cb_filled, b + 1)
                wait(dve, xb_done, TILES * b)
                for c in range(C):
                    last = v.tensor_scalar(cb[:, c, :], gc[:, P * c:P * (c + 1)], SPREAD, bvs[:, c:c + 1], ALU.mult, ALU.add)
                last.then_inc(cb_step, 1)
                dve.wait_ge(cb_step, 3 * b + 1)
                wait(dve, br_filled, b)
                v.tensor_copy(cb_hi[:, :, :], cb).then_inc(cb_step, 1)
                dve.wait_ge(cb_step, 3 * b + 2)
                v.tensor_tensor(cb_lo[:, :, :], cb, cb_hi[:, :, :].bitcast(F32), ALU.subtract).then_inc(cb_step, 1)

            def bias_row(b):
                dve.wait_ge(br_filled, b + 1)
                v.tensor_tensor(brow[:, :], gc[:, 0:D], bo[:, :], ALU.add).then_inc(brow_done, 1)

            def slot(b, t):
                now, part = parts(b, t)
                if part["op"]:
                    normalise(*part["op"])
                if part["ff"]:
                    norm2(*part["ff"])
                if part["mx"]:
                    row_max(*part["mx"], 0)
                if part["tqv"]:
                    xt_part(*part["tqv"])
                if part["mx"]:
                    row_max(*part["mx"], 1)
                if part["ff"]:
                    bb, tt = part["ff"]
                    n = TILES * bb + tt
                    dve.wait_ge(t2_hi_done, n + 1)
                    v.tensor_tensor(t2_lo[:, :, :], gb[:, 0:D].rearrange("p (c q) -> p c q", c=C),
                                    t2_hi[:, :, :].bitcast(F32), ALU.subtract).then_inc(t2_lo_done, 1)
                if part["mx"]:
                    row_max(*part["mx"], 2)
                if part["tqv"]:
                    qk_part(*part["tqv"], q_hi, q_lo, bq, q_hi_done, q_lo_done)
                if part["k"]:
                    qk_part(*part["k"], k_hi, k_lo, bk, k_hi_done, k_lo_done)
                if part["mx"]:
                    row_max(*part["mx"], 3)
                if part["ln"]:
                    stats1(*part["ln"])
                if part["op"]:
                    bb, tt = part["op"]
                    n = TILES * bb + tt
                    dve.wait_ge(ct_hi_done, n + 1)
                    v.tensor_tensor(ct_lo[:, :, :], gb[:, 0:D].rearrange("p (c q) -> p c q", c=C),
                                    ct_hi[:, :, :].bitcast(F32), ALU.subtract).then_inc(ct_lo_done, 1)
                if part["ff"]:
                    bb, tt = part["ff"]
                    i, _ = halves(tt)
                    dve.wait_ge(ff_filled, TILES * bb + tt + 1)
                    v.tensor_tensor(x2[:, i], ga[:, 0:D], x2[:, i], ALU.add).then_inc(y_done, 1)
                if part["ln"]:
                    norm1(*part["ln"])
                if part["mx"]:
                    row_max(*part["mx"], 4)
                if now and t == 2:
                    spread_bias(b)
                if part["mx"]:
                    row_max(*part["mx"], 5)
                if now and t == 2:
                    bias_row(b)
                if part["op"]:
                    bb, tt = part["op"]
                    i, m = halves(tt)
                    n = TILES * bb + tt
                    dve.wait_ge(op_filled, n + 1)
                    wait(dve, y_stored[i], 16 * (TILES // 2 * bb + m))
                    dve.wait_ge(xb_done, n + 1)
                    v.tensor_tensor(x2[:, i], ga[:, 0:D], xr[:, i], ALU.add).then_inc(x2_done, 1)
                    dve.wait_ge(x2_done, n + 1)
                    wait(dve, mv2_done, n)
                    v.bn_stats(st2[:, :], x2[:, i]).then_inc(bn2_done, 1)
                    dve.wait_ge(bn2_done, n + 1)
                    wait(dve, xn2_done, n)
                    settle(dve, n)
                    v.bn_aggr(mv2[:, :], st2[:, :]).then_inc(mv2_done, 1)

            def split_w(i, n):
                dve.wait_ge(w_hi_done, i + 1)
                v.tensor_tensor(w_lo[n][:, :, :], w_raw[n], w_hi[n][:, :, :].bitcast(F32),
                                ALU.subtract).then_inc(w_lo_done, 1)

            stats1(0, 0)
            split_w(0, "q")
            norm1(0, 0)
            for i, n in enumerate("kvo"):
                split_w(i + 1, n)
            dve.wait_ge(b_loaded, 64)
            v.scalar_tensor_tensor(bvs[:, :], bv[:, :], ROWS * SPREAD, bv[:, :], ALU.mult, ALU.add).then_inc(bvs_done, 1)
            stats1(0, 1)
            norm1(0, 1)
            xt_part(0, 0)
            qk_part(0, 0, q_hi, q_lo, bq, q_hi_done, q_lo_done)
            stats1(0, 2)
            qk_part(0, 0, k_hi, k_lo, bk, k_hi_done, k_lo_done)
            norm1(0, 2)
            dve.wait_ge(w_loaded["f"], 16)
            v.tensor_scalar(w_pos, w_raw["f"], 0.0, None, ALU.is_gt)
            v.tensor_scalar(w_neg, w_raw["f"], 0.0, None, ALU.is_lt).then_inc(w_sign_done, 1)
            dve.wait_ge(w_sign_done, 1)
            v.tensor_tensor(w_sign[:, :, :], w_pos, w_neg, ALU.subtract).then_inc(w_sign_done, 1)
            xt_part(0, 1)
            qk_part(0, 1, q_hi, q_lo, bq, q_hi_done, q_lo_done)
            qk_part(0, 1, k_hi, k_lo, bk, k_hi_done, k_lo_done)
            for f in range(MXF):
                row_max(0, 0, f)
            xt_part(0, 2)
            qk_part(0, 2, q_hi, q_lo, bq, q_hi_done, q_lo_done)
            for f in range(MXF):
                row_max(0, 1, f)
            for f in range(MXF):
                row_max(0, 2, f)
            dve.wait_ge(bvs_done, 1)
            run(dve, slot)

        @block.tensor
        def _(pe):
            mm = nc.tensor.matmul

            def products(dst, terms):
                terms = [(l(c), r(c)) for l, r in terms for c in range(C)]
                for j, (l, r) in enumerate(terms):
                    last = mm(dst, l, r, start=j == 0, stop=j == len(terms) - 1)
                return last

            def t1(b, p):
                n = PAIRS * b + p
                pe.wait_ge(xn_done, n + 1)
                if p == 0:
                    wait(pe, brow_done, b)
                else:
                    wait(pe, k_lo_done, n)
                for c in range(C):
                    for j in range(2):
                        last = nc.tensor.transpose(gc[:, 2 * P * c + P * j:2 * P * c + P * (j + 1)],
                                                   xn[:, j, P * c:P * (c + 1)], ident[:, :])
                last.then_inc(t1_filled, 1)

            def qk(b, p, w, filled):
                for m in range(C):
                    cols = slice(P * m, P * (m + 1))
                    last = products(gc[:, 2 * P * m:2 * P * (m + 1)],
                                    [(lambda c: w_hi[w][:, c, cols], lambda c: xt_hi[:, c, :]),
                                     (lambda c: w_hi[w][:, c, cols], lambda c: xt_lo[:, c, :]),
                                     (lambda c: w_lo[w][:, c, cols], lambda c: xt_hi[:, c, :])])
                last.then_inc(filled, 1)

            def q_proj(b, p):
                pe.wait_ge(xt_lo_done, PAIRS * b + p + 1)
                qk(b, p, "q", q_filled)

            def v_proj(b, p):
                pe.wait_ge(q_lo_done, PAIRS * b + p + 1)
                for j in range(2):
                    rows = slice(P * j, P * (j + 1))
                    last = products(gc[:, D * j:D * (j + 1)],
                                    [(lambda c: xt_hi[:, c, rows], lambda c: w_hi["v"][:, c, :]),
                                     (lambda c: xt_hi[:, c, rows], lambda c: w_lo["v"][:, c, :]),
                                     (lambda c: xt_lo[:, c, rows], lambda c: w_hi["v"][:, c, :])])
                last.then_inc(v_filled, 1)

            def k_proj(b, p):
                pe.wait_ge(v_done, PAIRS * b + p + 1)
                qk(b, p, "k", k_filled)

            def max_scores(b, t, f):
                rg, heads = MX_FILLS[f]
                n = MXF * (TILES * b + t) + f
                if f == 0 and t % 2 == 0:
                    i, m = halves(t // 2)
                    pe.wait_ge(q_stacked[i], 128 * (PAIRS // 2 * b + m + 1))
                    pe.wait_ge(k_stacked[i], 128 * (PAIRS // 2 * b + m + 1))
                wait(pe, mx_done, n)
                dst = mx_bank[:, 0:WIN * len(heads)].rearrange("p (h k) -> p h k", k=WIN)
                hs = slice(0, len(heads))
                if t == 0:
                    mm(dst, ident16[:, :], window0[:, hs, :], start=True, stop=False, skip_group_check=True)
                else:
                    mm(dst[:, :, 0:QB], ident16[:, :], window[:, hs, 0:QB], start=True, stop=False, skip_group_check=True)
                    mm(dst[:, :, P:WIN], ident16[:, :], window[:, hs, P:WIN], start=False, stop=False, skip_group_check=True)
                for j, h in enumerate(heads):
                    for blk in range(P // QB):
                        at = P * t + QB * blk
                        last = mm(mx_bank[QB * blk:QB * (blk + 1), WIN * j:WIN * (j + 1)],
                                  q_max[64 * rg:64 * rg + DK, h, at:at + QB],
                                  k_max[64 * rg:64 * rg + DK, h, at:at + WIN],
                                  start=False, stop=j == len(heads) - 1, skip_group_check=True)
                last.then_inc(mx_filled, 1)

            def turn_max(b, t):
                n = TILES * b + t
                pe.wait_ge(mx_done, MXF * (n + 1))
                wait(pe, ct_lo_done, n - 5)
                wait(pe, nm_done, n)
                nc.tensor.transpose(gb[0:H, 0:P], nmax[:, t % 2, :], ident[:, :]).then_inc(nm_filled, 1)

            def scores(b, t, f):
                n = TILES * b + t
                if f == 0:
                    for tt in ((0, 1) if t == 0 else (t + 1,) if t < TILES - 1 else ()):
                        i, m = halves(tt)
                        pe.wait_ge(nmax_stacked[i], 32 * (TILES // 2 * b + m + 1))
                wait(pe, exp_done, SC_FILLS * n + f - 1)
                q = 2 * P if t < TILES - 1 else P
                for j in range(2):
                    rg, h = divmod(2 * f + j, HB)
                    last = mm(sc_bank[f % 2][:, 2 * P * j:2 * P * j + q],
                              k_stack[64 * rg:64 * rg + SUMS, h, P * t:P * (t + 1)],
                              q_stack[64 * rg:64 * rg + SUMS, h, P * t:P * t + q], start=True, stop=True)
                last.then_inc(sc_filled, 1)

            def prob_v(b, t, f):
                n = TILES * b + t
                cg, nxt = divmod(f, 2)
                if nxt and t == TILES - 1:
                    return
                if f == 0:
                    pe.wait_ge(prob_masked, 2 * n + 1)
                    wait(pe, u_done, n)
                if f == 4:
                    pe.wait_ge(prob_masked, 2 * n + 2)
                for j in range(4):
                    h = 4 * cg + j
                    last = mm(pv_bank[(t + nxt) % 2][32 * j:32 * (j + 1), P * cg:P * (cg + 1)],
                              v_ones[:, t, h, :], prob[:, t % 2, h, P * nxt:P * (nxt + 1)],
                              start=cg == 0 and (nxt == 1 or t == 0), stop=cg == 3 and not nxt, skip_group_check=True)
                if f == (7 if t < TILES - 1 else 6):
                    last.then_inc(pv_filled, 1)

            def turn_u(b, t):
                n = TILES * b + t
                pe.wait_ge(u_done, n + 1)
                wait(pe, x2_done, n)
                for cg in range(4):
                    last = nc.tensor.transpose(ga[:, P * cg:P * (cg + 1)], u[:, t % 2, P * cg:P * (cg + 1)], ident[:, :])
                last.then_inc(ut_filled, 1)

            def turn_c(b, t):
                n = TILES * b + t
                pe.wait_ge(cx_done, n + 1)
                wait(pe, t2_lo_done, n)
                if isinstance(n, int) and n == 0:
                    pe.wait_ge(nm_done, 6)
                flat = cx[:, :, :].rearrange("p h d -> p (h d)")
                for c in range(C):
                    last = nc.tensor.transpose(gb[:, P * c:P * (c + 1)], flat[:, P * c:P * (c + 1)], ident[:, :])
                last.then_inc(ct_filled, 1)

            def o_proj(dst, hi, lo):
                return products(dst, [(lambda c: hi[:, c, :], lambda c: w_hi["o"][:, c, :]),
                                      (lambda c: hi[:, c, :], lambda c: w_lo["o"][:, c, :]),
                                      (lambda c: lo[:, c, :], lambda c: w_hi["o"][:, c, :])])

            def turn_x2(b, t, later):
                n = TILES * b + t
                pe.wait_ge(xn2_done, n + 1)
                if later:
                    pe.wait_ge(nm_done, n + 7)
                else:
                    pe.wait_ge(ct_lo_done, n + 1)
                for c in range(C):
                    last = nc.tensor.transpose(gb[:, P * c:P * (c + 1)], xn2[:, P * c:P * (c + 1)], ident[:, :])
                last.then_inc(t2_filled, 1)

            def slot(b, t):
                now, part = parts(b, t)
                if now:
                    scores(b, t, 0)
                if part["pv"]:
                    prob_v(*part["pv"], 0)
                if part["op"]:
                    turn_u(*part["op"])
                if part["nm"]:
                    turn_max(*part["nm"])
                if part["mx"]:
                    max_scores(*part["mx"], 0)
                if now:
                    scores(b, t, 1)
                if part["pv"]:
                    prob_v(*part["pv"], 1)
                if part["tqv"]:
                    t1(*part["tqv"])
                if part["mx"]:
                    max_scores(*part["mx"], 1)
                if now:
                    scores(b, t, 2)
                if part["pv"]:
                    prob_v(*part["pv"], 2)
                if part["ff"]:
                    turn_x2(*part["ff"], part["nm"])
                if part["mx"]:
                    max_scores(*part["mx"], 2)
                if now:
                    scores(b, t, 3)
                if part["pv"]:
                    prob_v(*part["pv"], 3)
                if part["tqv"]:
                    q_proj(*part["tqv"])
                if part["k"]:
                    k_proj(*part["k"])
                if part["mx"]:
                    max_scores(*part["mx"], 3)
                if now:
                    scores(b, t, 4)
                if part["pv"]:
                    prob_v(*part["pv"], 4)
                if part["op"]:
                    turn_c(*part["op"])
                if now:
                    scores(b, t, 5)
                if part["pv"]:
                    prob_v(*part["pv"], 5)
                if part["ff"]:
                    bb, tt = part["ff"]
                    n = TILES * bb + tt
                    pe.wait_ge(t2_lo_done, n + 1)
                    if part["op"]:
                        pe.wait_ge(cx_done, n + 2)
                    else:
                        pe.wait_ge(x2_done, n + 1)
                    products(ga[:, 0:D], [(lambda c: t2_hi[:, c, :], lambda c: w_sign[:, c, :]),
                                          (lambda c: t2_lo[:, c, :], lambda c: w_sign[:, c, :])]).then_inc(ff_filled, 1)
                if part["mx"]:
                    max_scores(*part["mx"], 4)
                if now:
                    scores(b, t, 6)
                if part["pv"]:
                    prob_v(*part["pv"], 6)
                if now and t == 2:
                    pe.wait_ge(vsum_step, TILES * (b + 1))
                    pe.wait_ge(k_lo_done, PAIRS * (b + 1))
                    for c in range(C):
                        last = mm(gc[:, P * c:P * (c + 1)], vsum[:, P * c:P * (c + 1)], ones[:, :], start=True, stop=True)
                    last.then_inc(cb_filled, 1)
                if part["mx"]:
                    max_scores(*part["mx"], 5)
                if now:
                    scores(b, t, 7)
                if part["pv"]:
                    prob_v(*part["pv"], 7)
                if now and t == 2:
                    pe.wait_ge(cb_step, 3 * (b + 1))
                    o_proj(gc[:, 0:D], cb_hi, cb_lo).then_inc(br_filled, 1)
                if part["op"]:
                    bb, tt = part["op"]
                    n = TILES * bb + tt
                    pe.wait_ge(ct_lo_done, n + 1)
                    wait(pe, y_done, n)
                    o_proj(ga[:, 0:D], ct_hi, ct_lo).then_inc(op_filled, 1)
                if part["tqv"]:
                    v_proj(*part["tqv"])

            pe.wait_ge(consts_done, 1)
            t1(0, 0)
            pe.wait_ge(w_lo_done, 4)
            q_proj(0, 0)
            v_proj(0, 0)
            k_proj(0, 0)
            t1(0, 1)
            q_proj(0, 1)
            v_proj(0, 1)
            k_proj(0, 1)
            for f in range(MXF):
                max_scores(0, 0, f)
            turn_max(0, 0)
            t1(0, 2)
            q_proj(0, 2)
            v_proj(0, 2)
            for f in range(MXF):
                max_scores(0, 1, f)
            turn_max(0, 1)
            for f in range(MXF):
                max_scores(0, 2, f)
            pe.wait_ge(w_sign_done, 2)
            run(pe, slot)


def kernel(L0_attn_x, L0_attn_Wq, L0_attn_bq, L0_attn_Wk, L0_attn_bk, L0_attn_Wv, L0_attn_bv, L0_attn_Wo,
           L0_attn_bo, L0_ffn_weight):
    import numpy as np
    import concourse.bacc as bacc
    from concourse.bass_utils import run_bass_kernel_spmd

    def by_place(w):
        w = np.asarray(w)
        return w.reshape(C, HB, DK, -1).transpose(0, 2, 1, 3).reshape(D, -1)

    def columns(v):
        return np.ascontiguousarray(np.asarray(v).reshape(C, P).T)

    arrays = {
        "x": np.asarray(L0_attn_x),
        "wq_t": by_place(L0_attn_Wq).T,
        "wk_t": by_place(L0_attn_Wk).T,
        "wv_t": np.asarray(L0_attn_Wv).T,
        "wo_t": np.asarray(L0_attn_Wo).T,
        "wf_t": np.asarray(L0_ffn_weight).T,
        "bq_c": columns(by_place(L0_attn_bq)),
        "bk_c": columns(by_place(L0_attn_bk)),
        "bv_c": columns(L0_attn_bv),
        "bo_r": np.broadcast_to(np.asarray(L0_attn_bo), (P, D)),
    }
    arrays = {k: np.ascontiguousarray(v) for k, v in arrays.items()}
    nc = bacc.Bacc("TRN2", target_bir_lowering=False, num_devices=1)
    args = {k: nc.dram_tensor(k, v.shape, mybir.dt.from_np(v.dtype), kind="ExternalInput").ap() for k, v in arrays.items()}
    out = nc.dram_tensor("out", arrays["x"].shape, F32, kind="ExternalOutput").ap()
    build(nc, out=out, **args)
    result = run_bass_kernel_spmd(nc, [arrays], core_ids=[0])
    return result.results[0]["out"]
```

```python
from contextlib import ExitStack

import concourse.bass as bass
from concourse import mybir

F32 = mybir.dt.float32
F32R = mybir.dt.float32r
BF16 = mybir.dt.bfloat16
ACT = mybir.ActivationFunctionType
ALU = mybir.AluOpType
AX = mybir.AxisListType

P = 128
H = 16
DK = 16
D = H * DK
C = D // P
HB = H // C
TILES = 8
PAIRS = TILES // 2
ROWS = TILES * P
QB = 32
WIN = QB + P
SCALE = 0.25
EPS = 1e-5
SPREAD = 1e-9
MASKED = -1e30
SUMS = 3 * DK + 1
SC_FILLS = 8
MX_FILLS = [(rg, heads) for heads in ((0, 1, 2), (3, 4, 5), (6, 7)) for rg in range(C)]
MXF = len(MX_FILLS)


def build(nc, x, wq_t, wk_t, wv_t, wo_t, wf_t, bq_c, bk_c, bv_c, bo_r, out):
    BATCHES = x.shape[0]
    LAST = BATCHES - 1
    NT = BATCHES * TILES
    x_pair = x.rearrange("b (g t p) d -> b g p t d", t=2, p=P)
    x_tile = x.rearrange("b (t p) d -> b t p d", p=P)
    y_tile = out.rearrange("b (t p) d -> b t p d", p=P)

    with ExitStack() as ctx:
        def sb(name, shape, dt=F32):
            return ctx.enter_context(nc.sbuf_tensor(name, shape, dt))

        def bank(name):
            return ctx.enter_context(nc.psum_tensor(name, [P, 512], F32))

        def sem(name):
            return ctx.enter_context(nc.semaphore(name))

        w_hi = {n: sb(f"wh_{n}", [P, C, D], F32R) for n in "qkvo"}
        w_lo = {n: sb(f"wl_{n}", [P, C, D], F32R) for n in "qkvo"}
        w_sign = sb("w_sign", [P, C, D], F32R)
        bq = sb("bq", [P, C])
        bk = sb("bk", [P, C])
        bv = sb("bv", [P, C])
        bvs = sb("bvs", [P, C])
        bo = sb("bo", [P, D])
        ident = sb("ident", [P, P])
        ident16 = sb("ident16", [P, P], BF16)
        ones = sb("ones", [P, P])
        window = sb("window", [P, 3, WIN], BF16)
        window0 = sb("window0", [P, 3, WIN], BF16)
        half = sb("half", [P, 2])
        xs = sb("xs", [P, 2, 2, D])
        st1 = sb("st1", [P, 2, 6])
        mv1 = sb("mv1", [P, 2, 2])
        ve1 = sb("ve1", [P, 2])
        rs1 = sb("rs1", [P, 2])
        xn = sb("xn", [P, 2, D])
        xt_hi = sb("xt_hi", [P, C, 2 * P], F32R)
        xt_lo = sb("xt_lo", [P, C, 2 * P], F32R)
        q_hi = sb("q_hi", [P, C, 2 * P], F32R)
        q_lo = sb("q_lo", [P, C, 2 * P], F32R)
        q_16 = sb("q_16", [P, C, 2 * P], BF16)
        k_hi = sb("k_hi", [P, C, 2 * P], F32R)
        k_lo = sb("k_lo", [P, C, 2 * P], F32R)
        k_16 = sb("k_16", [P, C, 2 * P], BF16)
        q_stack = sb("q_stack", [P, HB, ROWS], F32R)
        k_stack = sb("k_stack", [P, HB, ROWS], F32R)
        q_max = sb("q_max", [P, HB, ROWS], BF16)
        k_max = sb("k_max", [P, HB, P + ROWS], BF16)
        v_ones = sb("v_ones", [P, TILES, H, 2 * DK])
        vsum = sb("vsum", [P, D])
        nmax = sb("nmax", [P, 2, H])
        nmax_t = sb("nmax_t", [H, 2, P], F32R)
        prob = sb("prob", [P, 2, H, 2 * P])
        raw = prob[:, :, :, :].rearrange("p r h q -> p (r h q)").rearrange("p (n c d) -> p n c d", c=C, d=D)
        w_raw = {n: raw[:, i] for i, n in enumerate("qkvof")}
        w_pos, w_neg = raw[:, 5], raw[:, 6]
        u = sb("u", [P, 2, 512])
        rden = sb("rden", [P, H])
        cx = sb("cx", [P, H, DK])
        ct_hi = sb("ct_hi", [P, C, P], F32R)
        ct_lo = sb("ct_lo", [P, C, P], F32R)
        cb_hi = sb("cb_hi", [P, C, P], F32R)
        cb_lo = sb("cb_lo", [P, C, P], F32R)
        brow = sb("brow", [P, D])
        cb = brow[:, :].rearrange("p (c q) -> p c q", c=C)
        xr = sb("xr", [P, 2, D])
        x2 = sb("x2", [P, 2, D])
        st2 = sb("st2", [P, 6])
        mv2 = sb("mv2", [P, 2])
        ve2 = sb("ve2", [P, 1])
        rs2 = sb("rs2", [P, 1])
        xn2 = sb("xn2", [P, D])
        t2_hi = sb("t2_hi", [P, C, P], F32R)
        t2_lo = sb("t2_lo", [P, C, P], F32R)

        sc_bank = [bank("sc0"), bank("sc1")]
        mx_bank = bank("mx")
        pv_bank = [bank("pv0"), bank("pv1")]
        ga = bank("ga")
        gb = bank("gb")
        gc = bank("gc")

        w_loaded = {n: sem(f"w_loaded_{n}") for n in "qkvof"}
        b_loaded = sem("b_loaded")
        x_loaded = [sem("x_loaded0"), sem("x_loaded1")]
        q_stacked = [sem("q_stacked0"), sem("q_stacked1")]
        k_stacked = [sem("k_stacked0"), sem("k_stacked1")]
        q_max_set = [sem("q_max_set0"), sem("q_max_set1")]
        k_max_set = [sem("k_max_set0"), sem("k_max_set1")]
        nmax_stacked = [sem("nmax_stacked0"), sem("nmax_stacked1")]
        xr_loaded = [sem("xr_loaded0"), sem("xr_loaded1")]
        y_stored = [sem("y_stored0"), sem("y_stored1")]
        settled = {e: sem(f"settled_{n}") for n, e in (("sp", nc.sync.engine), ("pool", nc.gpsimd.engine), ("dve", nc.vector.engine))}
        consts_done = sem("consts_done")
        memset_done = sem("memset_done")
        pool_setup = sem("pool_setup")
        w_hi_done = sem("w_hi_done")
        w_lo_done = sem("w_lo_done")
        w_sign_done = sem("w_sign_done")
        bvs_done = sem("bvs_done")
        bn1_done, mv1_done, ve1_done, rs1_done, xn_done = map(sem, ("bn1_done", "mv1_done", "ve1_done", "rs1_done", "xn_done"))
        t1_filled, xt_hi_done, xt_lo_done = map(sem, ("t1_filled", "xt_hi_done", "xt_lo_done"))
        q_filled, q_hi_done, q_16_done, q_lo_done = map(sem, ("q_filled", "q_hi_done", "q_16_done", "q_lo_done"))
        k_filled, k_hi_done, k_16_done, k_lo_done = map(sem, ("k_filled", "k_hi_done", "k_16_done", "k_lo_done"))
        v_filled, v_done, vsum_step = map(sem, ("v_filled", "v_done", "vsum_step"))
        cb_filled, cb_step, br_filled, brow_done = map(sem, ("cb_filled", "cb_step", "br_filled", "brow_done"))
        sc_filled = sem("sc_filled")
        exp_done = sem("exp_done")
        prob_masked = sem("prob_masked")
        mx_filled = sem("mx_filled")
        mx_done = sem("mx_done")
        nm_filled, nm_done = map(sem, ("nm_filled", "nm_done"))
        pv_filled, u_done = map(sem, ("pv_filled", "u_done"))
        ut_filled, rden_done, cx_done = map(sem, ("ut_filled", "rden_done", "cx_done"))
        ct_filled, ct_hi_done, ct_lo_done = map(sem, ("ct_filled", "ct_hi_done", "ct_lo_done"))
        op_filled, xb_done, x2_done, bn2_done, mv2_done = map(sem, ("op_filled", "xb_done", "x2_done", "bn2_done", "mv2_done"))
        ve2_done, rs2_done, xn2_done = map(sem, ("ve2_done", "rs2_done", "xn2_done"))
        t2_filled, t2_hi_done, t2_lo_done = map(sem, ("t2_filled", "t2_hi_done", "t2_lo_done"))
        ff_filled, y_done = map(sem, ("ff_filled", "y_done"))

        def wait(eng, s, n):
            if not isinstance(n, int) or n > 0:
                eng.wait_ge(s, n)

        def settle(eng, n):
            if not isinstance(n, int):
                eng.sem_inc(settled[eng.engine], 1)

        def halves(t):
            return t % 2, t // 2

        def parts(b, t):
            def tile(shift):
                bb, tt = b + (t + shift) // TILES, (t + shift) % TILES
                if isinstance(b, int) and not 0 <= bb <= LAST:
                    return None
                return bb, tt

            def pair(shift):
                n = t + shift
                if n % 2:
                    return None
                bb, pp = b + n // TILES, n // 2 % PAIRS
                if isinstance(b, int) and not 0 <= bb <= LAST:
                    return None
                return bb, pp

            if isinstance(b, int) and b > LAST:
                now = None
            else:
                now = (b, t)
            return now, {"nm": tile(2), "mx": tile(3), "pv": tile(-1), "xr": tile(-2), "op": tile(-3), "ff": tile(-4),
                         "tqv": pair(5), "k": pair(4), "ln": pair(6), "load": pair(7)}

        def run(eng, slot):
            for t in range(TILES):
                slot(0, t)
            with eng.Fori(1, LAST) as b:
                for t in range(TILES):
                    slot(b, t)
            for t in range(TILES):
                slot(LAST, t)
            for t in range(4):
                slot(BATCHES, t)

        block = ctx.enter_context(nc.Block())

        @block.sync
        def _(sp):
            def load_x(b, p):
                i, n = halves(p)
                wait(sp, xn_done, PAIRS * b + p - 1)
                settle(sp, b)
                sp.dma_start(xs[:, i], x_pair[b, p]).then_inc(x_loaded[i], 16)

            def stack(b, p, hi, lo, b16, stack_, max_, shift, order, hi_done, lo_done, b16_done, stacked, max_set):
                i, _ = halves(p)
                cols = slice(2 * P * p, 2 * P * (p + 1))
                g = PAIRS * b + p
                wait(sp, sc_filled, SC_FILLS * (TILES * (b - 1) + 2 * p + 2))
                settle(sp, b)
                sp.wait_ge(b16_done, g + 1)
                settle(sp, g)
                for c in range(C):
                    sp.dma_start(max_[64 * c:64 * c + DK, :, shift + 2 * P * p:shift + 2 * P * (p + 1)],
                                 b16[:, c, :]).then_inc(max_set[i], 16)
                sp.wait_ge(hi_done, g + 1)
                sp.wait_ge(lo_done, g + 1)
                settle(sp, g)
                for c in range(C):
                    for r, part in enumerate(order):
                        src = (hi, lo)[part]
                        at = 64 * c + DK * r
                        sp.dma_start(stack_[at:at + DK, :, cols].bitcast(F32),
                                     src[:, c, :].bitcast(F32)).then_inc(stacked[i], 16)

            def stack_q(b, p):
                stack(b, p, q_hi, q_lo, q_16, q_stack, q_max, 0, (0, 0, 1), q_hi_done, q_lo_done, q_16_done, q_stacked, q_max_set)

            def stack_k(b, p):
                stack(b, p, k_hi, k_lo, k_16, k_stack, k_max, P, (0, 1, 0), k_hi_done, k_lo_done, k_16_done, k_stacked, k_max_set)

            def stack_nmax(b, t):
                i, _ = halves(t)
                sp.wait_ge(nm_done, TILES * b + t + 1)
                settle(sp, b)
                for c in range(C):
                    at = 64 * c + 3 * DK
                    sp.dma_start(q_stack[at:at + 1, :, P * t:P * (t + 1)].bitcast(F32),
                                 nmax_t[HB * c:HB * (c + 1), i, :].bitcast(F32)).then_inc(nmax_stacked[i], 16)

            def load_xr(b, t):
                i, _ = halves(t)
                wait(sp, x2_done, TILES * b + t - 1)
                settle(sp, b)
                sp.dma_start(xr[:, i], x_tile[b, t]).then_inc(xr_loaded[i], 16)

            def slot(b, t):
                now, part = parts(b, t)
                if part["nm"]:
                    stack_nmax(*part["nm"])
                if part["load"]:
                    load_x(*part["load"])
                if part["tqv"]:
                    stack_q(*part["tqv"])
                if part["k"]:
                    stack_k(*part["k"])
                if part["xr"]:
                    load_xr(*part["xr"])
                if part["ff"]:
                    bb, tt = part["ff"]
                    i, _ = halves(tt)
                    sp.wait_ge(y_done, TILES * bb + tt + 1)
                    settle(sp, bb)
                    sp.dma_start(y_tile[bb, tt], x2[:, i]).then_inc(y_stored[i], 16)

            load_x(0, 0)
            load_x(0, 1)
            sp.wait_ge(memset_done, 4)
            load_x(0, 2)
            stack_q(0, 0)
            stack_k(0, 0)
            load_x(0, 3)
            stack_q(0, 1)
            stack_k(0, 1)
            stack_nmax(0, 0)
            stack_q(0, 2)
            stack_nmax(0, 1)
            run(sp, slot)
            for i in range(2):
                sp.wait_ge(y_stored[i], 16 * (NT // 2))

        @block.gpsimd
        def _(pool):
            g = nc.gpsimd
            g.memset(half[:, :], -0.5)
            g.memset(ident[:, :], 0.0)
            g.memset(window[:, :, :], 0.0)
            g.memset(window0[:, :, :], 0.0).then_inc(pool_setup, 1)
            pool.wait_ge(pool_setup, 1)
            g.affine_select(out=ident[:, :], in_=ident[:, :], compare_op=ALU.not_equal, fill=1.0, base=0,
                            pattern=[[1, P]], channel_multiplier=-1).then_inc(pool_setup, 1)
            n = 2
            for mask in (window, window0):
                for blk in range(P // QB):
                    m = mask[QB * blk:QB * (blk + 1), :, :]
                    for base, cm, step in ((0, -1, 1), (P, 1, -1)):
                        pool.wait_ge(pool_setup, n)
                        g.affine_select(out=m, in_=m, compare_op=ALU.is_ge, fill=MASKED, base=base,
                                        pattern=[[0, 3], [step, WIN]], channel_multiplier=cm).then_inc(pool_setup, 1)
                        n += 1
            for blk in range(P // QB):
                m = window0[QB * blk:QB * (blk + 1), :, :]
                pool.wait_ge(pool_setup, n)
                g.affine_select(out=m, in_=m, compare_op=ALU.is_ge, fill=MASKED, base=QB * blk - P,
                                pattern=[[0, 3], [1, WIN]], channel_multiplier=0).then_inc(pool_setup, 1)
                n += 1
            pool.wait_ge(pool_setup, n)
            g.tensor_copy(ident16[:, :], ident[:, :]).then_inc(consts_done, 1)

            def rsqrt1(b, p):
                n = PAIRS * b + p
                pool.wait_ge(mv1_done, n + 1)
                settle(pool, n)
                g.tensor_scalar(ve1[:, :], mv1[:, :, 1], EPS, None, ALU.add).then_inc(ve1_done, 1)
                pool.wait_ge(ve1_done, n + 1)
                g.tensor_tensor(rs1[:, :], ve1[:, :], half[:, :], ALU.pow).then_inc(rs1_done, 1)

            def sum_v(b, p):
                pool.wait_ge(v_done, PAIRS * b + p + 1)
                for j in range(2):
                    n = TILES * b + 2 * p + j
                    v = v_ones[:, 2 * p + j, :, 0:DK]
                    s = vsum[:, :].rearrange("p (h d) -> p h d", h=H)
                    if p == 0 and j == 0:
                        wait(pool, cb_filled, b)
                        settle(pool, b)
                        g.tensor_copy(s, v).then_inc(vsum_step, 1)
                    else:
                        pool.wait_ge(vsum_step, n)
                        g.tensor_tensor(s, s, v, ALU.add).then_inc(vsum_step, 1)

            def mask_probs(b, t, r):
                n = TILES * b + t
                pool.wait_ge(exp_done, SC_FILLS * n + 4 * (r + 1))
                settle(pool, n)
                pr = prob[:, t % 2, HB * r:HB * (r + 1), :]
                if t < TILES - 1:
                    nxt = pr[:, :, P:2 * P]
                    g.affine_select(out=nxt, in_=nxt, compare_op=ALU.is_ge, fill=0.0, base=0,
                                    pattern=[[0, HB], [-1, P]], channel_multiplier=1)
                own = pr[:, :, 0:P]
                g.affine_select(out=own, in_=own, compare_op=ALU.is_ge, fill=0.0, base=0,
                                pattern=[[0, HB], [1, P]], channel_multiplier=-1).then_inc(prob_masked, 1)

            def add_biases(b, t):
                i, n = halves(t)
                pool.wait_ge(brow_done, b + 1)
                pool.wait_ge(xr_loaded[i], 16 * (TILES // 2 * b + n + 1))
                g.tensor_tensor(xr[:, i], xr[:, i], brow[:, :], ALU.add).then_inc(xb_done, 1)

            def rsqrt2(b, t):
                n = TILES * b + t
                pool.wait_ge(mv2_done, n + 1)
                settle(pool, n)
                g.tensor_scalar(ve2[:, :], mv2[:, 1:2], EPS, None, ALU.add).then_inc(ve2_done, 1)
                pool.wait_ge(ve2_done, n + 1)
                g.tensor_tensor(rs2[:, :], ve2[:, :], half[:, 0:1], ALU.pow).then_inc(rs2_done, 1)

            def slot(b, t):
                now, part = parts(b, t)
                if part["pv"]:
                    mask_probs(*part["pv"], 1)
                if part["k"]:
                    sum_v(*part["k"])
                if part["op"]:
                    add_biases(*part["op"])
                if now:
                    mask_probs(*now, 0)
                if part["ln"]:
                    rsqrt1(*part["ln"])
                if part["op"]:
                    rsqrt2(*part["op"])

            rsqrt1(0, 0)
            rsqrt1(0, 1)
            sum_v(0, 0)
            rsqrt1(0, 2)
            sum_v(0, 1)
            run(pool, slot)

        @block.scalar
        def _(act):
            a = nc.scalar
            for n, w in zip("qkvof", (wq_t, wk_t, wv_t, wo_t, wf_t)):
                act.dma_start(w_raw[n], w.rearrange("(c p) n -> p c n", p=P)).then_inc(w_loaded[n], 16)
                if n == "q":
                    for dst, src in ((bq, bq_c), (bk, bk_c), (bv, bv_c), (bo, bo_r)):
                        act.dma_start(dst[:, :], src).then_inc(b_loaded, 16)
            for n in "qkvo":
                act.wait_ge(w_loaded[n], 16)
                a.activation(w_hi[n][:, :, :], w_raw[n], ACT.Copy).then_inc(w_hi_done, 1)
            act.wait_ge(b_loaded, 64)

            def xt_part(b, p):
                n = PAIRS * b + p
                act.wait_ge(t1_filled, n + 1)
                wait(act, k_filled, n)
                a.activation(xt_hi[:, :, :], gc[:, :].rearrange("p (c q) -> p c q", c=C), ACT.Copy).then_inc(xt_hi_done, 1)

            def qk_part(b, p, filled, hi, b16, bias, hi_done, b16_done, stacked, max_set):
                n = PAIRS * b + p
                act.wait_ge(filled, n + 1)
                if not isinstance(n, int) or n > 0:
                    j = (p - 1) % 2
                    bb, pp = (b, p - 1) if p else (b - 1, PAIRS - 1)
                    act.wait_ge(max_set[j], 32 * (PAIRS // 2 * bb + pp // 2 + 1))
                    act.wait_ge(stacked[j], 96 * (PAIRS // 2 * bb + pp // 2 + 1))
                for c in range(C):
                    last = a.activation(hi[:, c, :], gc[:, 2 * P * c:2 * P * (c + 1)], ACT.Identity, bias=bias[:, c:c + 1])
                last.then_inc(hi_done, 1)
                act.wait_ge(hi_done, n + 1)
                a.activation(b16[:, :, :], hi[:, :, :].bitcast(F32), ACT.Copy).then_inc(b16_done, 1)

            def q_part(b, p):
                qk_part(b, p, q_filled, q_hi, q_16, bq, q_hi_done, q_16_done, q_stacked, q_max_set)

            def k_part(b, p):
                qk_part(b, p, k_filled, k_hi, k_16, bk, k_hi_done, k_16_done, k_stacked, k_max_set)

            def v_part(b, p):
                n = PAIRS * b + p
                act.wait_ge(v_filled, n + 1)
                wait(act, pv_filled, TILES * (b - 1) + 2 * p + 2)
                wait(act, vsum_step, TILES * b)
                a.activation(v_ones[:, 2 * p:2 * p + 2, :, 0:DK],
                             gc[:, :].rearrange("p (t h d) -> p t h d", t=2, h=H), ACT.Copy).then_inc(v_done, 1)

            def exp(b, t, f):
                n = TILES * b + t
                q = 2 * P if t < TILES - 1 else P
                act.wait_ge(sc_filled, SC_FILLS * n + f + 1)
                if f == 0:
                    wait(act, pv_filled, n - 1)
                    if isinstance(n, int) and n == 0:
                        act.wait_ge(w_lo_done, 4)
                        act.wait_ge(w_sign_done, 2)
                a.activation(prob[:, t % 2, 2 * f:2 * f + 2, 0:q],
                             sc_bank[f % 2][:, :].rearrange("p (h q) -> p h q", h=2)[:, :, 0:q],
                             ACT.Exp, scale=SCALE).then_inc(exp_done, 1)

            def nmax_part(b, t):
                i, m = halves(t)
                n = TILES * b + t
                act.wait_ge(nm_filled, n + 1)
                wait(act, nmax_stacked[i], 32 * (TILES // 2 * b + m))
                a.activation(nmax_t[:, i, :], gb[0:H, 0:P], ACT.Copy).then_inc(nm_done, 1)

            def slot(b, t):
                now, part = parts(b, t)
                if now:
                    exp(b, t, 0)
                if part["nm"]:
                    nmax_part(*part["nm"])
                if part["tqv"]:
                    xt_part(*part["tqv"])
                if now:
                    exp(b, t, 1)
                if now:
                    exp(b, t, 2)
                if part["ff"]:
                    bb, tt = part["ff"]
                    n = TILES * bb + tt
                    act.wait_ge(t2_filled, n + 1)
                    wait(act, ff_filled, n)
                    a.activation(t2_hi[:, :, :], gb[:, 0:D].rearrange("p (c q) -> p c q", c=C), ACT.Copy).then_inc(t2_hi_done, 1)
                if now:
                    exp(b, t, 3)
                if part["tqv"]:
                    q_part(*part["tqv"])
                if part["k"]:
                    k_part(*part["k"])
                if now:
                    exp(b, t, 4)
                if part["op"]:
                    bb, tt = part["op"]
                    n = TILES * bb + tt
                    act.wait_ge(ct_filled, n + 1)
                    wait(act, op_filled, n)
                    a.activation(ct_hi[:, :, :], gb[:, 0:D].rearrange("p (c q) -> p c q", c=C), ACT.Copy).then_inc(ct_hi_done, 1)
                if now:
                    exp(b, t, 5)
                    exp(b, t, 6)
                    exp(b, t, 7)
                if part["pv"]:
                    bb, tt = part["pv"]
                    n = TILES * bb + tt
                    act.wait_ge(pv_filled, n + 1)
                    wait(act, ut_filled, n - 1)
                    a.activation(u[:, tt % 2, :], pv_bank[tt % 2][:, :], ACT.Copy).then_inc(u_done, 1)
                if part["tqv"]:
                    v_part(*part["tqv"])

            def project(b, p):
                xt_part(b, p)
                q_part(b, p)
                v_part(b, p)

            act.wait_ge(memset_done, 5)
            project(0, 0)
            k_part(0, 0)
            project(0, 1)
            k_part(0, 1)
            nmax_part(0, 0)
            project(0, 2)
            nmax_part(0, 1)
            run(act, slot)

        @block.vector
        def _(dve):
            v = nc.vector
            v.memset(q_stack[:, :, :].bitcast(F32), 0.0).then_inc(memset_done, 1)
            v.memset(k_stack[:, :, :].bitcast(F32), 1.0).then_inc(memset_done, 1)
            v.memset(k_max[:, :, :], 0.0).then_inc(memset_done, 1)
            v.memset(q_max[:, :, :], 0.0).then_inc(memset_done, 1)
            v.memset(v_ones[:, :, :, :], 1.0).then_inc(memset_done, 1)
            v.memset(ones[:, :], 1.0)

            def stats1(b, p):
                i, m = halves(p)
                n = PAIRS * b + p
                dve.wait_ge(x_loaded[i], 16 * (PAIRS // 2 * b + m + 1))
                wait(dve, mv1_done, n)
                for j in range(2):
                    last = v.bn_stats(st1[:, j], xs[:, i, j])
                last.then_inc(bn1_done, 1)
                dve.wait_ge(bn1_done, n + 1)
                wait(dve, xn_done, n)
                settle(dve, n)
                for j in range(2):
                    last = v.bn_aggr(mv1[:, j], st1[:, j])
                last.then_inc(mv1_done, 1)

            def norm1(b, p):
                i, _ = halves(p)
                n = PAIRS * b + p
                dve.wait_ge(rs1_done, n + 1)
                wait(dve, t1_filled, n)
                for j in range(2):
                    last = v.tensor_scalar(xn[:, j], xs[:, i, j], mv1[:, j, 0:1], rs1[:, j:j + 1],
                                           ALU.subtract, ALU.mult)
                last.then_inc(xn_done, 1)

            def norm2(b, t):
                i, _ = halves(t)
                n = TILES * b + t
                dve.wait_ge(rs2_done, n + 1)
                wait(dve, t2_filled, n)
                v.tensor_scalar(xn2[:, :], x2[:, i], mv2[:, 0:1], rs2[:, :],
                                ALU.subtract, ALU.mult).then_inc(xn2_done, 1)

            def xt_part(b, p):
                n = PAIRS * b + p
                dve.wait_ge(xt_hi_done, n + 1)
                v.tensor_tensor(xt_lo[:, :, :], gc[:, :].rearrange("p (c q) -> p c q", c=C),
                                xt_hi[:, :, :].bitcast(F32), ALU.subtract).then_inc(xt_lo_done, 1)

            def qk_part(b, p, hi, lo, bias, hi_done, lo_done):
                dve.wait_ge(hi_done, PAIRS * b + p + 1)
                for c in range(C):
                    last = v.scalar_tensor_tensor(lo[:, c, :], gc[:, 2 * P * c:2 * P * (c + 1)], bias[:, c:c + 1],
                                                  hi[:, c, :].bitcast(F32), ALU.add, ALU.subtract)
                last.then_inc(lo_done, 1)

            def q_part(b, p):
                qk_part(b, p, q_hi, q_lo, bq, q_hi_done, q_lo_done)

            def k_part(b, p):
                qk_part(b, p, k_hi, k_lo, bk, k_hi_done, k_lo_done)

            def row_max(b, t, f):
                rg, heads = MX_FILLS[f]
                n = MXF * (TILES * b + t) + f
                dve.wait_ge(mx_filled, n + 1)
                if f == 0:
                    wait(dve, nm_filled, TILES * b + t - 1)
                h0 = HB * rg + heads[0]
                v.tensor_reduce(nmax[:, t % 2, h0:h0 + len(heads)],
                                mx_bank[:, 0:WIN * len(heads)].rearrange("p (h k) -> p h k", k=WIN),
                                AX.X, ALU.max, negate=True).then_inc(mx_done, 1)

            def normalise(b, t):
                n = TILES * b + t
                dve.wait_ge(ut_filled, n + 1)
                ut = ga[:, :].rearrange("p (h e) -> p h e", h=H)
                v.reciprocal(rden[:, :], ut[:, :, DK]).then_inc(rden_done, 1)
                dve.wait_ge(rden_done, n + 1)
                wait(dve, ct_filled, n)
                v.tensor_tensor(cx[:, :, :], ut[:, :, 0:DK], rden[:, :].unsqueeze(2).broadcast_to([P, H, DK]),
                                ALU.mult).then_inc(cx_done, 1)

            def spread_bias(b):
                dve.wait_ge(cb_filled, b + 1)
                wait(dve, xb_done, TILES * b)
                for c in range(C):
                    last = v.tensor_scalar(cb[:, c, :], gc[:, P * c:P * (c + 1)], SPREAD, bvs[:, c:c + 1], ALU.mult, ALU.add)
                last.then_inc(cb_step, 1)
                dve.wait_ge(cb_step, 3 * b + 1)
                wait(dve, br_filled, b)
                v.tensor_copy(cb_hi[:, :, :], cb).then_inc(cb_step, 1)
                dve.wait_ge(cb_step, 3 * b + 2)
                v.tensor_tensor(cb_lo[:, :, :], cb, cb_hi[:, :, :].bitcast(F32), ALU.subtract).then_inc(cb_step, 1)

            def bias_row(b):
                dve.wait_ge(br_filled, b + 1)
                v.tensor_tensor(brow[:, :], gc[:, 0:D], bo[:, :], ALU.add).then_inc(brow_done, 1)

            def slot(b, t):
                now, part = parts(b, t)
                if part["mx"]:
                    row_max(*part["mx"], 0)
                if part["ff"]:
                    norm2(*part["ff"])
                if part["tqv"]:
                    xt_part(*part["tqv"])
                if part["op"]:
                    normalise(*part["op"])
                if part["mx"]:
                    row_max(*part["mx"], 1)
                if part["ff"]:
                    bb, tt = part["ff"]
                    n = TILES * bb + tt
                    dve.wait_ge(t2_hi_done, n + 1)
                    v.tensor_tensor(t2_lo[:, :, :], gb[:, 0:D].rearrange("p (c q) -> p c q", c=C),
                                    t2_hi[:, :, :].bitcast(F32), ALU.subtract).then_inc(t2_lo_done, 1)
                if part["mx"]:
                    row_max(*part["mx"], 2)
                if part["mx"]:
                    row_max(*part["mx"], 3)
                if part["tqv"]:
                    q_part(*part["tqv"])
                if part["k"]:
                    k_part(*part["k"])
                if part["ff"]:
                    bb, tt = part["ff"]
                    i, _ = halves(tt)
                    dve.wait_ge(ff_filled, TILES * bb + tt + 1)
                    v.tensor_tensor(x2[:, i], ga[:, 0:D], x2[:, i], ALU.add).then_inc(y_done, 1)
                if part["op"]:
                    bb, tt = part["op"]
                    n = TILES * bb + tt
                    dve.wait_ge(ct_hi_done, n + 1)
                    v.tensor_tensor(ct_lo[:, :, :], gb[:, 0:D].rearrange("p (c q) -> p c q", c=C),
                                    ct_hi[:, :, :].bitcast(F32), ALU.subtract).then_inc(ct_lo_done, 1)
                if part["mx"]:
                    row_max(*part["mx"], 4)
                if part["ln"]:
                    stats1(*part["ln"])
                if now and t == 2:
                    spread_bias(b)
                if part["op"]:
                    bb, tt = part["op"]
                    i, m = halves(tt)
                    n = TILES * bb + tt
                    dve.wait_ge(op_filled, n + 1)
                    wait(dve, y_stored[i], 16 * (TILES // 2 * bb + m))
                    dve.wait_ge(xb_done, n + 1)
                    v.tensor_tensor(x2[:, i], ga[:, 0:D], xr[:, i], ALU.add).then_inc(x2_done, 1)
                if part["mx"]:
                    row_max(*part["mx"], 5)
                if part["op"]:
                    dve.wait_ge(x2_done, n + 1)
                    wait(dve, mv2_done, n)
                    v.bn_stats(st2[:, :], x2[:, i]).then_inc(bn2_done, 1)
                    dve.wait_ge(bn2_done, n + 1)
                    wait(dve, xn2_done, n)
                    settle(dve, n)
                    v.bn_aggr(mv2[:, :], st2[:, :]).then_inc(mv2_done, 1)
                if part["ln"]:
                    norm1(*part["ln"])
                if now and t == 2:
                    bias_row(b)

            def split_w(i, n):
                dve.wait_ge(w_hi_done, i + 1)
                v.tensor_tensor(w_lo[n][:, :, :], w_raw[n], w_hi[n][:, :, :].bitcast(F32),
                                ALU.subtract).then_inc(w_lo_done, 1)

            stats1(0, 0)
            split_w(0, "q")
            norm1(0, 0)
            for i, n in enumerate("kvo"):
                split_w(i + 1, n)
            dve.wait_ge(b_loaded, 64)
            v.scalar_tensor_tensor(bvs[:, :], bv[:, :], ROWS * SPREAD, bv[:, :], ALU.mult, ALU.add).then_inc(bvs_done, 1)
            stats1(0, 1)
            norm1(0, 1)
            xt_part(0, 0)
            q_part(0, 0)
            stats1(0, 2)
            k_part(0, 0)
            norm1(0, 2)
            dve.wait_ge(w_loaded["f"], 16)
            v.tensor_scalar(w_pos, w_raw["f"], 0.0, None, ALU.is_gt)
            v.tensor_scalar(w_neg, w_raw["f"], 0.0, None, ALU.is_lt).then_inc(w_sign_done, 1)
            dve.wait_ge(w_sign_done, 1)
            v.tensor_tensor(w_sign[:, :, :], w_pos, w_neg, ALU.subtract).then_inc(w_sign_done, 1)
            xt_part(0, 1)
            q_part(0, 1)
            k_part(0, 1)
            for f in range(MXF):
                row_max(0, 0, f)
            xt_part(0, 2)
            q_part(0, 2)
            for f in range(MXF):
                row_max(0, 1, f)
            for f in range(MXF):
                row_max(0, 2, f)
            dve.wait_ge(bvs_done, 1)
            run(dve, slot)

        @block.tensor
        def _(pe):
            mm = nc.tensor.matmul

            def products(dst, terms):
                terms = [(l(c), r(c)) for l, r in terms for c in range(C)]
                for j, (l, r) in enumerate(terms):
                    last = mm(dst, l, r, start=j == 0, stop=j == len(terms) - 1)
                return last

            def t1(b, p):
                n = PAIRS * b + p
                pe.wait_ge(xn_done, n + 1)
                if p == 0:
                    wait(pe, brow_done, b)
                else:
                    wait(pe, k_lo_done, n)
                for c in range(C):
                    for j in range(2):
                        last = nc.tensor.transpose(gc[:, 2 * P * c + P * j:2 * P * c + P * (j + 1)],
                                                   xn[:, j, P * c:P * (c + 1)], ident[:, :])
                last.then_inc(t1_filled, 1)

            def qk(m, w, filled):
                cols = slice(P * m, P * (m + 1))
                last = products(gc[:, 2 * P * m:2 * P * (m + 1)],
                                [(lambda c: w_hi[w][:, c, cols], lambda c: xt_hi[:, c, :]),
                                 (lambda c: w_hi[w][:, c, cols], lambda c: xt_lo[:, c, :]),
                                 (lambda c: w_lo[w][:, c, cols], lambda c: xt_hi[:, c, :])])
                if m == C - 1:
                    last.then_inc(filled, 1)

            def q_proj(b, p, m):
                if m == 0:
                    pe.wait_ge(xt_lo_done, PAIRS * b + p + 1)
                qk(m, "q", q_filled)

            def v_proj(b, p, j):
                if j == 0:
                    pe.wait_ge(q_lo_done, PAIRS * b + p + 1)
                rows = slice(P * j, P * (j + 1))
                last = products(gc[:, D * j:D * (j + 1)],
                                [(lambda c: xt_hi[:, c, rows], lambda c: w_hi["v"][:, c, :]),
                                 (lambda c: xt_hi[:, c, rows], lambda c: w_lo["v"][:, c, :]),
                                 (lambda c: xt_lo[:, c, rows], lambda c: w_hi["v"][:, c, :])])
                if j == 1:
                    last.then_inc(v_filled, 1)

            def k_proj(b, p, m):
                if m == 0:
                    pe.wait_ge(v_done, PAIRS * b + p + 1)
                qk(m, "k", k_filled)

            def max_scores(b, t, f):
                rg, heads = MX_FILLS[f]
                n = MXF * (TILES * b + t) + f
                if f == 0 and t % 2 == 0:
                    i, m = halves(t // 2)
                    pe.wait_ge(q_max_set[i], 32 * (PAIRS // 2 * b + m + 1))
                    pe.wait_ge(k_max_set[i], 32 * (PAIRS // 2 * b + m + 1))
                wait(pe, mx_done, n)
                dst = mx_bank[:, 0:WIN * len(heads)].rearrange("p (h k) -> p h k", k=WIN)
                hs = slice(0, len(heads))
                if t == 0:
                    mm(dst, ident16[:, :], window0[:, hs, :], start=True, stop=False, skip_group_check=True)
                else:
                    mm(dst[:, :, 0:QB], ident16[:, :], window[:, hs, 0:QB], start=True, stop=False, skip_group_check=True)
                    mm(dst[:, :, P:WIN], ident16[:, :], window[:, hs, P:WIN], start=False, stop=False, skip_group_check=True)
                for j, h in enumerate(heads):
                    for blk in range(P // QB):
                        at = P * t + QB * blk
                        last = mm(mx_bank[QB * blk:QB * (blk + 1), WIN * j:WIN * (j + 1)],
                                  q_max[64 * rg:64 * rg + DK, h, at:at + QB],
                                  k_max[64 * rg:64 * rg + DK, h, at:at + WIN],
                                  start=False, stop=j == len(heads) - 1, skip_group_check=True)
                last.then_inc(mx_filled, 1)

            def turn_max(b, t):
                n = TILES * b + t
                pe.wait_ge(mx_done, MXF * (n + 1))
                wait(pe, ct_lo_done, n - 5)
                wait(pe, nm_done, n)
                nc.tensor.transpose(gb[0:H, 0:P], nmax[:, t % 2, :], ident[:, :]).then_inc(nm_filled, 1)

            def scores(b, t, f):
                n = TILES * b + t
                if f == 0:
                    for tt in ((0, 1) if t == 0 else (t + 1,) if t < TILES - 1 else ()):
                        i, m = halves(tt)
                        pe.wait_ge(nmax_stacked[i], 32 * (TILES // 2 * b + m + 1))
                        if tt % 2 == 0:
                            i, m = halves(tt // 2)
                            pe.wait_ge(q_stacked[i], 96 * (PAIRS // 2 * b + m + 1))
                            pe.wait_ge(k_stacked[i], 96 * (PAIRS // 2 * b + m + 1))
                wait(pe, exp_done, SC_FILLS * n + f - 1)
                q = 2 * P if t < TILES - 1 else P
                for j in range(2):
                    rg, h = divmod(2 * f + j, HB)
                    last = mm(sc_bank[f % 2][:, 2 * P * j:2 * P * j + q],
                              k_stack[64 * rg:64 * rg + SUMS, h, P * t:P * (t + 1)],
                              q_stack[64 * rg:64 * rg + SUMS, h, P * t:P * t + q], start=True, stop=True)
                last.then_inc(sc_filled, 1)

            def prob_v(b, t, f):
                n = TILES * b + t
                cg, nxt = divmod(f, 2)
                if nxt and t == TILES - 1:
                    return
                if f == 0:
                    pe.wait_ge(prob_masked, 2 * n + 1)
                    if t == 0:
                        wait(pe, u_done, n - 1)
                if f == 1:
                    wait(pe, u_done, n)
                if f == 4:
                    pe.wait_ge(prob_masked, 2 * n + 2)
                for j in range(4):
                    h = 4 * cg + j
                    last = mm(pv_bank[(t + nxt) % 2][32 * j:32 * (j + 1), P * cg:P * (cg + 1)],
                              v_ones[:, t, h, :], prob[:, t % 2, h, P * nxt:P * (nxt + 1)],
                              start=cg == 0 and (nxt == 1 or t == 0), stop=cg == 3 and not nxt, skip_group_check=True)
                if f == (7 if t < TILES - 1 else 6):
                    last.then_inc(pv_filled, 1)

            def turn_u(b, t):
                n = TILES * b + t
                pe.wait_ge(u_done, n + 1)
                wait(pe, x2_done, n)
                for cg in range(4):
                    last = nc.tensor.transpose(ga[:, P * cg:P * (cg + 1)], u[:, t % 2, P * cg:P * (cg + 1)], ident[:, :])
                last.then_inc(ut_filled, 1)

            def turn_c(b, t):
                n = TILES * b + t
                pe.wait_ge(cx_done, n + 1)
                wait(pe, t2_lo_done, n)
                if isinstance(n, int) and n == 0:
                    pe.wait_ge(nm_done, 6)
                flat = cx[:, :, :].rearrange("p h d -> p (h d)")
                for c in range(C):
                    last = nc.tensor.transpose(gb[:, P * c:P * (c + 1)], flat[:, P * c:P * (c + 1)], ident[:, :])
                last.then_inc(ct_filled, 1)

            def o_proj(dst, hi, lo):
                return products(dst, [(lambda c: hi[:, c, :], lambda c: w_hi["o"][:, c, :]),
                                      (lambda c: hi[:, c, :], lambda c: w_lo["o"][:, c, :]),
                                      (lambda c: lo[:, c, :], lambda c: w_hi["o"][:, c, :])])

            def turn_x2(b, t, later):
                n = TILES * b + t
                pe.wait_ge(xn2_done, n + 1)
                if later:
                    pe.wait_ge(nm_done, n + 7)
                else:
                    pe.wait_ge(ct_lo_done, n + 1)
                for c in range(C):
                    last = nc.tensor.transpose(gb[:, P * c:P * (c + 1)], xn2[:, P * c:P * (c + 1)], ident[:, :])
                last.then_inc(t2_filled, 1)

            def second_layer(b, t, later):
                n = TILES * b + t
                pe.wait_ge(t2_lo_done, n + 1)
                if later:
                    pe.wait_ge(cx_done, n + 2)
                else:
                    pe.wait_ge(x2_done, n + 1)
                products(ga[:, 0:D], [(lambda c: t2_hi[:, c, :], lambda c: w_sign[:, c, :]),
                                      (lambda c: t2_lo[:, c, :], lambda c: w_sign[:, c, :])]).then_inc(ff_filled, 1)

            def sum_bias(b):
                pe.wait_ge(vsum_step, TILES * (b + 1))
                pe.wait_ge(k_lo_done, PAIRS * (b + 1))
                for c in range(C):
                    last = mm(gc[:, P * c:P * (c + 1)], vsum[:, P * c:P * (c + 1)], ones[:, :], start=True, stop=True)
                last.then_inc(cb_filled, 1)

            def out_proj(b, t):
                n = TILES * b + t
                pe.wait_ge(ct_lo_done, n + 1)
                wait(pe, y_done, n)
                o_proj(ga[:, 0:D], ct_hi, ct_lo).then_inc(op_filled, 1)

            def slot(b, t):
                now, part = parts(b, t)
                op, ff, tqv, k, mx, pv = (part[n] for n in ("op", "ff", "tqv", "k", "mx", "pv"))
                if now:
                    scores(b, t, 0)
                if op:
                    turn_u(*op)
                if part["nm"]:
                    turn_max(*part["nm"])
                if mx:
                    max_scores(*mx, 0)
                if tqv:
                    t1(*tqv)
                if pv:
                    prob_v(*pv, 0)
                if now:
                    scores(b, t, 1)
                if k:
                    k_proj(*k, 0)
                if mx:
                    max_scores(*mx, 1)
                if pv:
                    prob_v(*pv, 1)
                if now:
                    scores(b, t, 2)
                if ff:
                    turn_x2(*ff, part["nm"])
                if tqv:
                    q_proj(*tqv, 0)
                if mx:
                    max_scores(*mx, 2)
                if pv:
                    prob_v(*pv, 2)
                if now:
                    scores(b, t, 3)
                if tqv:
                    q_proj(*tqv, 1)
                if k:
                    k_proj(*k, 1)
                if mx:
                    max_scores(*mx, 3)
                if pv:
                    prob_v(*pv, 3)
                if now:
                    scores(b, t, 4)
                if op:
                    turn_c(*op)
                if ff:
                    second_layer(*ff, op)
                if pv:
                    prob_v(*pv, 4)
                if now:
                    scores(b, t, 5)
                if tqv:
                    v_proj(*tqv, 0)
                if now and t == 2:
                    sum_bias(b)
                if mx:
                    max_scores(*mx, 4)
                if pv:
                    prob_v(*pv, 5)
                if now:
                    scores(b, t, 6)
                if op:
                    out_proj(*op)
                if mx:
                    max_scores(*mx, 5)
                if pv:
                    prob_v(*pv, 6)
                if now:
                    scores(b, t, 7)
                if tqv:
                    v_proj(*tqv, 1)
                if now and t == 2:
                    pe.wait_ge(cb_step, 3 * (b + 1))
                    o_proj(gc[:, 0:D], cb_hi, cb_lo).then_inc(br_filled, 1)
                if pv:
                    prob_v(*pv, 7)

            def both(proj, b, p):
                for m in range(2):
                    proj(b, p, m)

            pe.wait_ge(consts_done, 1)
            t1(0, 0)
            pe.wait_ge(w_lo_done, 4)
            both(q_proj, 0, 0)
            both(v_proj, 0, 0)
            both(k_proj, 0, 0)
            t1(0, 1)
            both(q_proj, 0, 1)
            both(v_proj, 0, 1)
            both(k_proj, 0, 1)
            for f in range(MXF):
                max_scores(0, 0, f)
            turn_max(0, 0)
            t1(0, 2)
            both(q_proj, 0, 2)
            both(v_proj, 0, 2)
            for f in range(MXF):
                max_scores(0, 1, f)
            turn_max(0, 1)
            for f in range(MXF):
                max_scores(0, 2, f)
            pe.wait_ge(w_sign_done, 2)
            run(pe, slot)


def kernel(L0_attn_x, L0_attn_Wq, L0_attn_bq, L0_attn_Wk, L0_attn_bk, L0_attn_Wv, L0_attn_bv, L0_attn_Wo,
           L0_attn_bo, L0_ffn_weight):
    import numpy as np
    import concourse.bacc as bacc
    from concourse.bass_utils import run_bass_kernel_spmd

    def by_place(w):
        w = np.asarray(w)
        return w.reshape(C, HB, DK, -1).transpose(0, 2, 1, 3).reshape(D, -1)

    def columns(v):
        return np.ascontiguousarray(np.asarray(v).reshape(C, P).T)

    arrays = {
        "x": np.asarray(L0_attn_x),
        "wq_t": by_place(L0_attn_Wq).T,
        "wk_t": by_place(L0_attn_Wk).T,
        "wv_t": np.asarray(L0_attn_Wv).T,
        "wo_t": np.asarray(L0_attn_Wo).T,
        "wf_t": np.asarray(L0_ffn_weight).T,
        "bq_c": columns(by_place(L0_attn_bq)),
        "bk_c": columns(by_place(L0_attn_bk)),
        "bv_c": columns(L0_attn_bv),
        "bo_r": np.broadcast_to(np.asarray(L0_attn_bo), (P, D)),
    }
    arrays = {k: np.ascontiguousarray(v) for k, v in arrays.items()}
    nc = bacc.Bacc("TRN2", target_bir_lowering=False, num_devices=1)
    args = {k: nc.dram_tensor(k, v.shape, mybir.dt.from_np(v.dtype), kind="ExternalInput").ap() for k, v in arrays.items()}
    out = nc.dram_tensor("out", arrays["x"].shape, F32, kind="ExternalOutput").ap()
    build(nc, out=out, **args)
    result = run_bass_kernel_spmd(nc, [arrays], core_ids=[0])
    return result.results[0]["out"]
```

```python
from contextlib import ExitStack

import concourse.bass as bass
from concourse import mybir

F32 = mybir.dt.float32
F32R = mybir.dt.float32r
BF16 = mybir.dt.bfloat16
ACT = mybir.ActivationFunctionType
ALU = mybir.AluOpType
AX = mybir.AxisListType

P = 128
H = 16
DK = 16
D = H * DK
C = D // P
HB = H // C
TILES = 8
PAIRS = TILES // 2
ROWS = TILES * P
QB = 32
WIN = QB + P
SCALE = 0.25
EPS = 1e-5
SPREAD = 1e-9
MASKED = -1e30
SUMS = 3 * DK + 1
SC_FILLS = 8
MX_FILLS = [(rg, heads) for heads in ((0, 1, 2), (3, 4, 5), (6, 7)) for rg in range(C)]
MXF = len(MX_FILLS)


def build(nc, x, wq_t, wk_t, wv_t, wo_t, wf_t, bq_c, bk_c, bv_c, bo_r, out):
    BATCHES = x.shape[0]
    LAST = BATCHES - 1
    NT = BATCHES * TILES
    x_pair = x.rearrange("b (g t p) d -> b g p t d", t=2, p=P)
    x_tile = x.rearrange("b (t p) d -> b t p d", p=P)
    y_tile = out.rearrange("b (t p) d -> b t p d", p=P)

    with ExitStack() as ctx:
        def sb(name, shape, dt=F32):
            return ctx.enter_context(nc.sbuf_tensor(name, shape, dt))

        def bank(name):
            return ctx.enter_context(nc.psum_tensor(name, [P, 512], F32))

        def sem(name):
            return ctx.enter_context(nc.semaphore(name))

        w_hi = {n: sb(f"wh_{n}", [P, C, D], F32R) for n in "qkvo"}
        w_lo = {n: sb(f"wl_{n}", [P, C, D], F32R) for n in "qkvo"}
        w_sign = sb("w_sign", [P, C, D], F32R)
        bq = sb("bq", [P, C])
        bk = sb("bk", [P, C])
        bv = sb("bv", [P, C])
        bvs = sb("bvs", [P, C])
        bo = sb("bo", [P, D])
        ident = sb("ident", [P, P])
        ident16 = sb("ident16", [P, P], BF16)
        ones = sb("ones", [P, P])
        window = sb("window", [P, 3, WIN], BF16)
        window0 = sb("window0", [P, 3, WIN], BF16)
        half = sb("half", [P, 2])
        xs = sb("xs", [P, 2, 2, D])
        st1 = sb("st1", [P, 2, 6])
        mv1 = sb("mv1", [P, 2, 2])
        ve1 = sb("ve1", [P, 2])
        rs1 = sb("rs1", [P, 2])
        xn = sb("xn", [P, 2, D])
        xt_hi = sb("xt_hi", [P, C, 2 * P], F32R)
        xt_lo = sb("xt_lo", [P, C, 2 * P], F32R)
        q_hi = sb("q_hi", [P, C, 2 * P], F32R)
        q_lo = sb("q_lo", [P, C, 2 * P], F32R)
        q_16 = sb("q_16", [P, C, 2 * P], BF16)
        k_hi = sb("k_hi", [P, C, 2 * P], F32R)
        k_lo = sb("k_lo", [P, C, 2 * P], F32R)
        k_16 = sb("k_16", [P, C, 2 * P], BF16)
        q_stack = sb("q_stack", [P, HB, ROWS], F32R)
        k_stack = sb("k_stack", [P, HB, ROWS], F32R)
        q_max = sb("q_max", [P, HB, ROWS], BF16)
        k_max = sb("k_max", [P, HB, P + ROWS], BF16)
        v_ones = sb("v_ones", [P, TILES, H, 2 * DK])
        vsum = sb("vsum", [P, D])
        nmax = sb("nmax", [P, 2, H])
        nmax_t = sb("nmax_t", [H, 2, P], F32R)
        prob = sb("prob", [P, 2, H, 2 * P])
        raw = prob[:, :, :, :].rearrange("p r h q -> p (r h q)").rearrange("p (n c d) -> p n c d", c=C, d=D)
        w_raw = {n: raw[:, i] for i, n in enumerate("qkvof")}
        w_pos, w_neg = raw[:, 5], raw[:, 6]
        u = sb("u", [P, 2, 512])
        rden = sb("rden", [P, H])
        cx = sb("cx", [P, H, DK])
        ct_hi = sb("ct_hi", [P, C, P], F32R)
        ct_lo = sb("ct_lo", [P, C, P], F32R)
        cb_hi = sb("cb_hi", [P, C, P], F32R)
        cb_lo = sb("cb_lo", [P, C, P], F32R)
        brow = sb("brow", [P, D])
        cb = brow[:, :].rearrange("p (c q) -> p c q", c=C)
        xr = sb("xr", [P, 2, D])
        x2 = sb("x2", [P, 2, D])
        st2 = sb("st2", [P, 6])
        mv2 = sb("mv2", [P, 2])
        ve2 = sb("ve2", [P, 1])
        rs2 = sb("rs2", [P, 1])
        xn2 = sb("xn2", [P, D])
        t2_hi = sb("t2_hi", [P, C, P], F32R)
        t2_lo = sb("t2_lo", [P, C, P], F32R)

        sc_bank = [bank("sc0"), bank("sc1")]
        mx_bank = bank("mx")
        pv_bank = [bank("pv0"), bank("pv1")]
        ga = bank("ga")
        gb = bank("gb")
        gc = bank("gc")

        w_loaded = {n: sem(f"w_loaded_{n}") for n in "qkvof"}
        b_loaded = sem("b_loaded")
        x_loaded = [sem("x_loaded0"), sem("x_loaded1")]
        q_stacked = [sem("q_stacked0"), sem("q_stacked1")]
        k_stacked = [sem("k_stacked0"), sem("k_stacked1")]
        q_max_set = [sem("q_max_set0"), sem("q_max_set1")]
        k_max_set = [sem("k_max_set0"), sem("k_max_set1")]
        nmax_stacked = [sem("nmax_stacked0"), sem("nmax_stacked1")]
        xr_loaded = [sem("xr_loaded0"), sem("xr_loaded1")]
        y_stored = [sem("y_stored0"), sem("y_stored1")]
        settled = {e: sem(f"settled_{n}") for n, e in (("sp", nc.sync.engine), ("pool", nc.gpsimd.engine), ("dve", nc.vector.engine))}
        consts_done = sem("consts_done")
        memset_done = sem("memset_done")
        ones_done = sem("ones_done")
        ones_stacked = sem("ones_stacked")
        windows_done = sem("windows_done")
        pool_setup = sem("pool_setup")
        w_hi_done = sem("w_hi_done")
        w_lo_done = sem("w_lo_done")
        w_sign_done = sem("w_sign_done")
        bvs_done = sem("bvs_done")
        bn1_done, mv1_done, ve1_done, rs1_done, xn_done = map(sem, ("bn1_done", "mv1_done", "ve1_done", "rs1_done", "xn_done"))
        t1_filled, xt_hi_done, xt_lo_done = map(sem, ("t1_filled", "xt_hi_done", "xt_lo_done"))
        q_filled, q_hi_done, q_16_done, q_lo_done = map(sem, ("q_filled", "q_hi_done", "q_16_done", "q_lo_done"))
        k_filled, k_hi_done, k_16_done, k_lo_done = map(sem, ("k_filled", "k_hi_done", "k_16_done", "k_lo_done"))
        v_filled, v_done, vsum_step = map(sem, ("v_filled", "v_done", "vsum_step"))
        cb_filled, cb_step, br_filled, brow_done = map(sem, ("cb_filled", "cb_step", "br_filled", "brow_done"))
        sc_filled = sem("sc_filled")
        exp_done = sem("exp_done")
        prob_masked = sem("prob_masked")
        mx_filled = sem("mx_filled")
        mx_done = sem("mx_done")
        nm_filled, nm_done = map(sem, ("nm_filled", "nm_done"))
        pv_filled, u_done = map(sem, ("pv_filled", "u_done"))
        ut_filled, rden_done, cx_done = map(sem, ("ut_filled", "rden_done", "cx_done"))
        ct_filled, ct_hi_done, ct_lo_done = map(sem, ("ct_filled", "ct_hi_done", "ct_lo_done"))
        op_filled, xb_done, x2_done, bn2_done, mv2_done = map(sem, ("op_filled", "xb_done", "x2_done", "bn2_done", "mv2_done"))
        ve2_done, rs2_done, xn2_done = map(sem, ("ve2_done", "rs2_done", "xn2_done"))
        t2_filled, t2_hi_done, t2_lo_done = map(sem, ("t2_filled", "t2_hi_done", "t2_lo_done"))
        ff_filled, y_done = map(sem, ("ff_filled", "y_done"))

        def wait(eng, s, n):
            if not isinstance(n, int) or n > 0:
                eng.wait_ge(s, n)

        def settle(eng, n):
            if not isinstance(n, int):
                eng.sem_inc(settled[eng.engine], 1)

        def halves(t):
            return t % 2, t // 2

        def parts(b, t):
            def tile(shift):
                bb, tt = b + (t + shift) // TILES, (t + shift) % TILES
                if isinstance(b, int) and not 0 <= bb <= LAST:
                    return None
                return bb, tt

            def pair(shift):
                n = t + shift
                if n % 2:
                    return None
                bb, pp = b + n // TILES, n // 2 % PAIRS
                if isinstance(b, int) and not 0 <= bb <= LAST:
                    return None
                return bb, pp

            if isinstance(b, int) and b > LAST:
                now = None
            else:
                now = (b, t)
            return now, {"nm": tile(2), "mx": tile(3), "pv": tile(-1), "xr": tile(-2), "op": tile(-3), "ff": tile(-4),
                         "tqv": pair(5), "k": pair(4), "ln": pair(6), "load": pair(7)}

        def run(eng, slot):
            for t in range(TILES):
                slot(0, t)
            with eng.Fori(1, LAST) as b:
                for t in range(TILES):
                    slot(b, t)
            for t in range(TILES):
                slot(LAST, t)
            for t in range(4):
                slot(BATCHES, t)

        block = ctx.enter_context(nc.Block())

        @block.sync
        def _(sp):
            def load_x(b, p):
                i, n = halves(p)
                wait(sp, xn_done, PAIRS * b + p - 1)
                settle(sp, b)
                sp.dma_start(xs[:, i], x_pair[b, p]).then_inc(x_loaded[i], 16)

            def stack(b, p, hi, lo, b16, stack_, max_, shift, order, hi_done, lo_done, b16_done, stacked, max_set):
                i, _ = halves(p)
                cols = slice(2 * P * p, 2 * P * (p + 1))
                g = PAIRS * b + p
                wait(sp, sc_filled, SC_FILLS * (TILES * (b - 1) + 2 * p + 2))
                settle(sp, b)
                sp.wait_ge(b16_done, g + 1)
                settle(sp, g)
                for c in range(C):
                    sp.dma_start(max_[64 * c:64 * c + DK, :, shift + 2 * P * p:shift + 2 * P * (p + 1)],
                                 b16[:, c, :]).then_inc(max_set[i], 16)
                sp.wait_ge(hi_done, g + 1)
                sp.wait_ge(lo_done, g + 1)
                settle(sp, g)
                for c in range(C):
                    for r, part in enumerate(order):
                        src = (hi, lo)[part]
                        at = 64 * c + DK * r
                        sp.dma_start(stack_[at:at + DK, :, cols].bitcast(F32),
                                     src[:, c, :].bitcast(F32)).then_inc(stacked[i], 16)

            def stack_q(b, p):
                stack(b, p, q_hi, q_lo, q_16, q_stack, q_max, 0, (0, 0, 1), q_hi_done, q_lo_done, q_16_done, q_stacked, q_max_set)

            def stack_k(b, p):
                stack(b, p, k_hi, k_lo, k_16, k_stack, k_max, P, (0, 1, 0), k_hi_done, k_lo_done, k_16_done, k_stacked, k_max_set)

            def stack_nmax(b, t):
                i, _ = halves(t)
                sp.wait_ge(nm_done, TILES * b + t + 1)
                settle(sp, b)
                for c in range(C):
                    at = 64 * c + 3 * DK
                    sp.dma_start(q_stack[at:at + 1, :, P * t:P * (t + 1)].bitcast(F32),
                                 nmax_t[HB * c:HB * (c + 1), i, :].bitcast(F32)).then_inc(nmax_stacked[i], 16)

            def load_xr(b, t):
                i, _ = halves(t)
                wait(sp, x2_done, TILES * b + t - 1)
                settle(sp, b)
                sp.dma_start(xr[:, i], x_tile[b, t]).then_inc(xr_loaded[i], 16)

            def slot(b, t):
                now, part = parts(b, t)
                if part["nm"]:
                    stack_nmax(*part["nm"])
                if part["load"]:
                    load_x(*part["load"])
                if part["tqv"]:
                    stack_q(*part["tqv"])
                if part["k"]:
                    stack_k(*part["k"])
                if part["xr"]:
                    load_xr(*part["xr"])
                if part["ff"]:
                    bb, tt = part["ff"]
                    i, _ = halves(tt)
                    sp.wait_ge(y_done, TILES * bb + tt + 1)
                    settle(sp, bb)
                    sp.dma_start(y_tile[bb, tt], x2[:, i]).then_inc(y_stored[i], 16)

            load_x(0, 0)
            load_x(0, 1)
            sp.wait_ge(ones_done, 1)
            for c in range(C):
                at = 64 * c + 3 * DK
                sp.dma_start(k_stack[at:at + 1, :, :].bitcast(F32), ones[0:HB * ROWS // P, :]).then_inc(ones_stacked, 16)
            load_x(0, 2)
            stack_q(0, 0)
            stack_k(0, 0)
            load_x(0, 3)
            stack_q(0, 1)
            stack_nmax(0, 0)
            stack_k(0, 1)
            stack_nmax(0, 1)
            stack_q(0, 2)
            run(sp, slot)
            for i in range(2):
                sp.wait_ge(y_stored[i], 16 * (NT // 2))

        @block.gpsimd
        def _(pool):
            g = nc.gpsimd
            g.memset(half[:, :], -0.5)
            g.memset(ident[:, :], 0.0).then_inc(pool_setup, 1)
            pool.wait_ge(pool_setup, 1)
            g.affine_select(out=ident[:, :], in_=ident[:, :], compare_op=ALU.not_equal, fill=1.0, base=0,
                            pattern=[[1, P]], channel_multiplier=-1).then_inc(pool_setup, 1)
            pool.wait_ge(pool_setup, 2)
            g.tensor_copy(ident16[:, :], ident[:, :]).then_inc(consts_done, 1)
            g.memset(window[:, 0, :], 0.0)
            g.memset(window0[:, 0, :], 0.0).then_inc(pool_setup, 1)
            g.memset(k_max[:, :, 0:P], 0.0).then_inc(memset_done, 1)

            def make_windows():
                n = 3
                for mask in (window, window0):
                    for blk in range(P // QB):
                        m = mask[QB * blk:QB * (blk + 1), 0, :]
                        for base, cm, step in ((0, -1, 1), (P, 1, -1)):
                            pool.wait_ge(pool_setup, n)
                            g.affine_select(out=m, in_=m, compare_op=ALU.is_ge, fill=MASKED, base=base,
                                            pattern=[[step, WIN]], channel_multiplier=cm).then_inc(pool_setup, 1)
                            n += 1
                for blk in range(P // QB):
                    m = window0[QB * blk:QB * (blk + 1), 0, :]
                    pool.wait_ge(pool_setup, n)
                    g.affine_select(out=m, in_=m, compare_op=ALU.is_ge, fill=MASKED, base=QB * blk - P,
                                    pattern=[[1, WIN]], channel_multiplier=0).then_inc(pool_setup, 1)
                    n += 1
                pool.wait_ge(pool_setup, n)
                for mask in (window, window0):
                    for h in (1, 2):
                        last = g.tensor_copy(mask[:, h, :], mask[:, 0, :])
                last.then_inc(windows_done, 1)

            def rsqrt1(b, p):
                n = PAIRS * b + p
                pool.wait_ge(mv1_done, n + 1)
                settle(pool, n)
                g.tensor_scalar(ve1[:, :], mv1[:, :, 1], EPS, None, ALU.add).then_inc(ve1_done, 1)
                pool.wait_ge(ve1_done, n + 1)
                g.tensor_tensor(rs1[:, :], ve1[:, :], half[:, :], ALU.pow).then_inc(rs1_done, 1)

            def sum_v(b, p):
                pool.wait_ge(v_done, PAIRS * b + p + 1)
                for j in range(2):
                    n = TILES * b + 2 * p + j
                    v = v_ones[:, 2 * p + j, :, 0:DK]
                    s = vsum[:, :].rearrange("p (h d) -> p h d", h=H)
                    if p == 0 and j == 0:
                        wait(pool, cb_filled, b)
                        settle(pool, b)
                        g.tensor_copy(s, v).then_inc(vsum_step, 1)
                    else:
                        pool.wait_ge(vsum_step, n)
                        g.tensor_tensor(s, s, v, ALU.add).then_inc(vsum_step, 1)

            def mask_probs(b, t, r):
                n = TILES * b + t
                pool.wait_ge(exp_done, SC_FILLS * n + 4 * (r + 1))
                settle(pool, n)
                pr = prob[:, t % 2, HB * r:HB * (r + 1), :]
                if t < TILES - 1:
                    nxt = pr[:, :, P:2 * P]
                    g.affine_select(out=nxt, in_=nxt, compare_op=ALU.is_ge, fill=0.0, base=0,
                                    pattern=[[0, HB], [-1, P]], channel_multiplier=1)
                own = pr[:, :, 0:P]
                g.affine_select(out=own, in_=own, compare_op=ALU.is_ge, fill=0.0, base=0,
                                pattern=[[0, HB], [1, P]], channel_multiplier=-1).then_inc(prob_masked, 1)

            def add_biases(b, t):
                i, n = halves(t)
                pool.wait_ge(brow_done, b + 1)
                pool.wait_ge(xr_loaded[i], 16 * (TILES // 2 * b + n + 1))
                g.tensor_tensor(xr[:, i], xr[:, i], brow[:, :], ALU.add).then_inc(xb_done, 1)

            def rsqrt2(b, t):
                n = TILES * b + t
                pool.wait_ge(mv2_done, n + 1)
                settle(pool, n)
                g.tensor_scalar(ve2[:, :], mv2[:, 1:2], EPS, None, ALU.add).then_inc(ve2_done, 1)
                pool.wait_ge(ve2_done, n + 1)
                g.tensor_tensor(rs2[:, :], ve2[:, :], half[:, 0:1], ALU.pow).then_inc(rs2_done, 1)

            def slot(b, t):
                now, part = parts(b, t)
                if part["pv"]:
                    mask_probs(*part["pv"], 1)
                if part["k"]:
                    sum_v(*part["k"])
                if part["op"]:
                    add_biases(*part["op"])
                if part["ln"]:
                    rsqrt1(*part["ln"])
                if now:
                    mask_probs(*now, 0)
                if part["op"]:
                    rsqrt2(*part["op"])

            rsqrt1(0, 0)
            rsqrt1(0, 1)
            make_windows()
            rsqrt1(0, 2)
            sum_v(0, 0)
            sum_v(0, 1)
            run(pool, slot)

        @block.scalar
        def _(act):
            a = nc.scalar
            for n, w in zip("qvkof", (wq_t, wv_t, wk_t, wo_t, wf_t)):
                act.dma_start(w_raw[n], w.rearrange("(c p) n -> p c n", p=P)).then_inc(w_loaded[n], 16)
                if n == "q":
                    for dst, src in ((bq, bq_c), (bk, bk_c), (bv, bv_c), (bo, bo_r)):
                        act.dma_start(dst[:, :], src).then_inc(b_loaded, 16)

            def w_part(n):
                act.wait_ge(w_loaded[n], 16)
                a.activation(w_hi[n][:, :, :], w_raw[n], ACT.Copy).then_inc(w_hi_done, 1)

            def xt_part(b, p, bank=gc):
                n = PAIRS * b + p
                act.wait_ge(t1_filled, n + 1)
                wait(act, k_filled, n)
                a.activation(xt_hi[:, :, :], bank[:, :].rearrange("p (c q) -> p c q", c=C), ACT.Copy).then_inc(xt_hi_done, 1)

            def qk_part(b, p, bank, filled, hi, bias, hi_done, stacked, max_set):
                n = PAIRS * b + p
                act.wait_ge(filled, n + 1)
                if not isinstance(n, int) or n > 0:
                    j = (p - 1) % 2
                    bb, pp = (b, p - 1) if p else (b - 1, PAIRS - 1)
                    act.wait_ge(max_set[j], 32 * (PAIRS // 2 * bb + pp // 2 + 1))
                    act.wait_ge(stacked[j], 96 * (PAIRS // 2 * bb + pp // 2 + 1))
                for c in range(C):
                    last = a.activation(hi[:, c, :], bank[:, 2 * P * c:2 * P * (c + 1)], ACT.Identity, bias=bias[:, c:c + 1])
                last.then_inc(hi_done, 1)

            def bf16_part(b, p, hi, b16, hi_done, b16_done):
                act.wait_ge(hi_done, PAIRS * b + p + 1)
                a.activation(b16[:, :, :], hi[:, :, :].bitcast(F32), ACT.Copy).then_inc(b16_done, 1)

            def q_part(b, p, bank=gc):
                qk_part(b, p, bank, q_filled, q_hi, bq, q_hi_done, q_stacked, q_max_set)

            def q_16_part(b, p):
                bf16_part(b, p, q_hi, q_16, q_hi_done, q_16_done)

            def k_part(b, p, bank=gc):
                qk_part(b, p, bank, k_filled, k_hi, bk, k_hi_done, k_stacked, k_max_set)

            def k_16_part(b, p):
                bf16_part(b, p, k_hi, k_16, k_hi_done, k_16_done)

            def v_part(b, p, bank=gc):
                n = PAIRS * b + p
                act.wait_ge(v_filled, n + 1)
                wait(act, pv_filled, TILES * (b - 1) + 2 * p + 2)
                wait(act, vsum_step, TILES * b)
                a.activation(v_ones[:, 2 * p:2 * p + 2, :, 0:DK],
                             bank[:, :].rearrange("p (t h d) -> p t h d", t=2, h=H), ACT.Copy).then_inc(v_done, 1)

            def exp(b, t, f):
                n = TILES * b + t
                q = 2 * P if t < TILES - 1 else P
                act.wait_ge(sc_filled, SC_FILLS * n + f + 1)
                if f == 0:
                    wait(act, pv_filled, n - 1)
                    if isinstance(n, int) and n == 0:
                        act.wait_ge(w_lo_done, 4)
                        act.wait_ge(w_sign_done, 2)
                a.activation(prob[:, t % 2, 2 * f:2 * f + 2, 0:q],
                             sc_bank[f % 2][:, :].rearrange("p (h q) -> p h q", h=2)[:, :, 0:q],
                             ACT.Exp, scale=SCALE).then_inc(exp_done, 1)

            def nmax_part(b, t):
                i, m = halves(t)
                n = TILES * b + t
                act.wait_ge(nm_filled, n + 1)
                wait(act, nmax_stacked[i], 32 * (TILES // 2 * b + m))
                a.activation(nmax_t[:, i, :], gb[0:H, 0:P], ACT.Copy).then_inc(nm_done, 1)

            def slot(b, t):
                now, part = parts(b, t)
                if now:
                    exp(b, t, 0)
                if part["nm"]:
                    nmax_part(*part["nm"])
                if part["tqv"]:
                    xt_part(*part["tqv"])
                if now:
                    exp(b, t, 1)
                if now:
                    exp(b, t, 2)
                if part["ff"]:
                    bb, tt = part["ff"]
                    n = TILES * bb + tt
                    act.wait_ge(t2_filled, n + 1)
                    wait(act, ff_filled, n)
                    a.activation(t2_hi[:, :, :], gb[:, 0:D].rearrange("p (c q) -> p c q", c=C), ACT.Copy).then_inc(t2_hi_done, 1)
                if now:
                    exp(b, t, 3)
                if part["tqv"]:
                    q_part(*part["tqv"])
                if part["k"]:
                    k_part(*part["k"])
                if now:
                    exp(b, t, 4)
                if part["op"]:
                    bb, tt = part["op"]
                    n = TILES * bb + tt
                    act.wait_ge(ct_filled, n + 1)
                    wait(act, op_filled, n)
                    a.activation(ct_hi[:, :, :], gb[:, 0:D].rearrange("p (c q) -> p c q", c=C), ACT.Copy).then_inc(ct_hi_done, 1)
                if part["tqv"]:
                    q_16_part(*part["tqv"])
                if part["k"]:
                    k_16_part(*part["k"])
                if now:
                    exp(b, t, 5)
                    exp(b, t, 6)
                    exp(b, t, 7)
                if part["pv"]:
                    bb, tt = part["pv"]
                    n = TILES * bb + tt
                    act.wait_ge(pv_filled, n + 1)
                    wait(act, ut_filled, n - 1)
                    a.activation(u[:, tt % 2, :], pv_bank[tt % 2][:, :], ACT.Copy).then_inc(u_done, 1)
                if part["tqv"]:
                    v_part(*part["tqv"])

            w_part("q")
            xt_part(0, 0, sc_bank[0])
            for n in "vko":
                w_part(n)
            act.wait_ge(b_loaded, 64)
            for p in range(2):
                if p > 0:
                    xt_part(0, p, sc_bank[p % 2])
                q_part(0, p)
                q_16_part(0, p)
                v_part(0, p, ga)
                k_part(0, p, gb)
                k_16_part(0, p)
            xt_part(0, 2, sc_bank[0])
            nmax_part(0, 0)
            nmax_part(0, 1)
            q_part(0, 2)
            q_16_part(0, 2)
            v_part(0, 2, ga)
            run(act, slot)

        @block.vector
        def _(dve):
            v = nc.vector
            v.memset(ones[:, :], 1.0).then_inc(ones_done, 1)
            v.memset(v_ones[:, :, :, DK:], 1.0).then_inc(memset_done, 1)

            def stats1(b, p):
                i, m = halves(p)
                n = PAIRS * b + p
                dve.wait_ge(x_loaded[i], 16 * (PAIRS // 2 * b + m + 1))
                wait(dve, mv1_done, n)
                for j in range(2):
                    last = v.bn_stats(st1[:, j], xs[:, i, j])
                last.then_inc(bn1_done, 1)
                dve.wait_ge(bn1_done, n + 1)
                wait(dve, xn_done, n)
                settle(dve, n)
                for j in range(2):
                    last = v.bn_aggr(mv1[:, j], st1[:, j])
                last.then_inc(mv1_done, 1)

            def norm1(b, p):
                i, _ = halves(p)
                n = PAIRS * b + p
                dve.wait_ge(rs1_done, n + 1)
                wait(dve, t1_filled, n)
                for j in range(2):
                    last = v.tensor_scalar(xn[:, j], xs[:, i, j], mv1[:, j, 0:1], rs1[:, j:j + 1],
                                           ALU.subtract, ALU.mult)
                last.then_inc(xn_done, 1)

            def norm2(b, t):
                i, _ = halves(t)
                n = TILES * b + t
                dve.wait_ge(rs2_done, n + 1)
                wait(dve, t2_filled, n)
                v.tensor_scalar(xn2[:, :], x2[:, i], mv2[:, 0:1], rs2[:, :],
                                ALU.subtract, ALU.mult).then_inc(xn2_done, 1)

            def xt_part(b, p, bank=gc):
                n = PAIRS * b + p
                dve.wait_ge(xt_hi_done, n + 1)
                v.tensor_tensor(xt_lo[:, :, :], bank[:, :].rearrange("p (c q) -> p c q", c=C),
                                xt_hi[:, :, :].bitcast(F32), ALU.subtract).then_inc(xt_lo_done, 1)

            def qk_part(b, p, bank, hi, lo, bias, hi_done, lo_done):
                dve.wait_ge(hi_done, PAIRS * b + p + 1)
                for c in range(C):
                    last = v.scalar_tensor_tensor(lo[:, c, :], bank[:, 2 * P * c:2 * P * (c + 1)], bias[:, c:c + 1],
                                                  hi[:, c, :].bitcast(F32), ALU.add, ALU.subtract)
                last.then_inc(lo_done, 1)

            def q_part(b, p, bank=gc):
                qk_part(b, p, bank, q_hi, q_lo, bq, q_hi_done, q_lo_done)

            def k_part(b, p, bank=gc):
                qk_part(b, p, bank, k_hi, k_lo, bk, k_hi_done, k_lo_done)

            def row_max(b, t, f, bank=mx_bank):
                rg, heads = MX_FILLS[f]
                n = MXF * (TILES * b + t) + f
                dve.wait_ge(mx_filled, n + 1)
                if f == 0:
                    wait(dve, nm_filled, TILES * b + t - 1)
                h0 = HB * rg + heads[0]
                v.tensor_reduce(nmax[:, t % 2, h0:h0 + len(heads)],
                                bank[:, 0:WIN * len(heads)].rearrange("p (h k) -> p h k", k=WIN),
                                AX.X, ALU.max, negate=True).then_inc(mx_done, 1)

            def normalise(b, t):
                n = TILES * b + t
                dve.wait_ge(ut_filled, n + 1)
                ut = ga[:, :].rearrange("p (h e) -> p h e", h=H)
                v.reciprocal(rden[:, :], ut[:, :, DK]).then_inc(rden_done, 1)
                dve.wait_ge(rden_done, n + 1)
                wait(dve, ct_filled, n)
                v.tensor_tensor(cx[:, :, :], ut[:, :, 0:DK], rden[:, :].unsqueeze(2).broadcast_to([P, H, DK]),
                                ALU.mult).then_inc(cx_done, 1)

            def spread_bias(b):
                dve.wait_ge(cb_filled, b + 1)
                wait(dve, xb_done, TILES * b)
                for c in range(C):
                    last = v.tensor_scalar(cb[:, c, :], gc[:, P * c:P * (c + 1)], SPREAD, bvs[:, c:c + 1], ALU.mult, ALU.add)
                last.then_inc(cb_step, 1)
                dve.wait_ge(cb_step, 3 * b + 1)
                wait(dve, br_filled, b)
                v.tensor_copy(cb_hi[:, :, :], cb).then_inc(cb_step, 1)
                dve.wait_ge(cb_step, 3 * b + 2)
                v.tensor_tensor(cb_lo[:, :, :], cb, cb_hi[:, :, :].bitcast(F32), ALU.subtract).then_inc(cb_step, 1)

            def bias_row(b):
                dve.wait_ge(br_filled, b + 1)
                v.tensor_tensor(brow[:, :], gb[:, 0:D], bo[:, :], ALU.add).then_inc(brow_done, 1)

            def slot(b, t):
                now, part = parts(b, t)
                if part["mx"]:
                    row_max(*part["mx"], 0)
                if part["ff"]:
                    norm2(*part["ff"])
                if part["tqv"]:
                    xt_part(*part["tqv"])
                if part["mx"]:
                    row_max(*part["mx"], 1)
                if part["op"]:
                    normalise(*part["op"])
                if part["ff"]:
                    bb, tt = part["ff"]
                    n = TILES * bb + tt
                    dve.wait_ge(t2_hi_done, n + 1)
                    v.tensor_tensor(t2_lo[:, :, :], gb[:, 0:D].rearrange("p (c q) -> p c q", c=C),
                                    t2_hi[:, :, :].bitcast(F32), ALU.subtract).then_inc(t2_lo_done, 1)
                if part["mx"]:
                    row_max(*part["mx"], 2)
                if part["ln"]:
                    stats1(*part["ln"])
                if now and t == 3:
                    bias_row(b)
                if part["mx"]:
                    row_max(*part["mx"], 3)
                if part["tqv"]:
                    q_part(*part["tqv"])
                if part["k"]:
                    k_part(*part["k"])
                if part["op"]:
                    bb, tt = part["op"]
                    n = TILES * bb + tt
                    dve.wait_ge(ct_hi_done, n + 1)
                    v.tensor_tensor(ct_lo[:, :, :], gb[:, 0:D].rearrange("p (c q) -> p c q", c=C),
                                    ct_hi[:, :, :].bitcast(F32), ALU.subtract).then_inc(ct_lo_done, 1)
                if part["ff"]:
                    bb, tt = part["ff"]
                    i, _ = halves(tt)
                    dve.wait_ge(ff_filled, TILES * bb + tt + 1)
                    v.tensor_tensor(x2[:, i], ga[:, 0:D], x2[:, i], ALU.add).then_inc(y_done, 1)
                if part["mx"]:
                    row_max(*part["mx"], 4)
                if part["ln"]:
                    norm1(*part["ln"])
                if part["op"]:
                    bb, tt = part["op"]
                    i, m = halves(tt)
                    n = TILES * bb + tt
                    dve.wait_ge(op_filled, n + 1)
                    wait(dve, y_stored[i], 16 * (TILES // 2 * bb + m))
                    dve.wait_ge(xb_done, n + 1)
                    v.tensor_tensor(x2[:, i], ga[:, 0:D], xr[:, i], ALU.add).then_inc(x2_done, 1)
                if part["mx"]:
                    row_max(*part["mx"], 5)
                if now and t == 2:
                    spread_bias(b)
                if part["op"]:
                    dve.wait_ge(x2_done, n + 1)
                    wait(dve, mv2_done, n)
                    v.bn_stats(st2[:, :], x2[:, i]).then_inc(bn2_done, 1)
                    dve.wait_ge(bn2_done, n + 1)
                    wait(dve, xn2_done, n)
                    settle(dve, n)
                    v.bn_aggr(mv2[:, :], st2[:, :]).then_inc(mv2_done, 1)

            def split_w(i, n):
                dve.wait_ge(w_hi_done, i + 1)
                v.tensor_tensor(w_lo[n][:, :, :], w_raw[n], w_hi[n][:, :, :].bitcast(F32),
                                ALU.subtract).then_inc(w_lo_done, 1)

            for p in range(2):
                stats1(0, p)
                norm1(0, p)
            split_w(0, "q")
            xt_part(0, 0, sc_bank[0])
            for i, n in enumerate("vk"):
                split_w(i + 1, n)
            q_part(0, 0)
            stats1(0, 2)
            k_part(0, 0, gb)
            split_w(3, "o")
            xt_part(0, 1, sc_bank[1])
            norm1(0, 2)
            q_part(0, 1)
            dve.wait_ge(b_loaded, 64)
            v.scalar_tensor_tensor(bvs[:, :], bv[:, :], ROWS * SPREAD, bv[:, :], ALU.mult, ALU.add).then_inc(bvs_done, 1)
            dve.wait_ge(w_loaded["f"], 16)
            v.tensor_scalar(w_pos, w_raw["f"], 0.0, None, ALU.is_gt)
            v.tensor_scalar(w_neg, w_raw["f"], 0.0, None, ALU.is_lt).then_inc(w_sign_done, 1)
            k_part(0, 1, gb)
            dve.wait_ge(w_sign_done, 1)
            v.tensor_tensor(w_sign[:, :, :], w_pos, w_neg, ALU.subtract).then_inc(w_sign_done, 1)
            for t in range(3):
                for f in range(MXF):
                    row_max(0, t, f, (mx_bank, pv_bank[0])[f % 2])
                if t == 0:
                    xt_part(0, 2, sc_bank[0])
                if t == 1:
                    q_part(0, 2)
            dve.wait_ge(bvs_done, 1)
            run(dve, slot)

        @block.tensor
        def _(pe):
            mm = nc.tensor.matmul

            def products(dst, terms):
                terms = [(l(c), r(c)) for l, r in terms for c in range(C)]
                for j, (l, r) in enumerate(terms):
                    last = mm(dst, l, r, start=j == 0, stop=j == len(terms) - 1)
                return last

            def t1(b, p, bank=gc):
                n = PAIRS * b + p
                pe.wait_ge(xn_done, n + 1)
                if bank is gc:
                    if p == 0:
                        pe.wait_ge(cb_step, 3 * b - 2)
                    else:
                        pe.wait_ge(k_lo_done, n)
                for c in range(C):
                    for j in range(2):
                        last = nc.tensor.transpose(bank[:, 2 * P * c + P * j:2 * P * c + P * (j + 1)],
                                                   xn[:, j, P * c:P * (c + 1)], ident[:, :])
                last.then_inc(t1_filled, 1)

            def qk(m, w, filled, bank):
                cols = slice(P * m, P * (m + 1))
                last = products(bank[:, 2 * P * m:2 * P * (m + 1)],
                                [(lambda c: w_hi[w][:, c, cols], lambda c: xt_hi[:, c, :]),
                                 (lambda c: w_hi[w][:, c, cols], lambda c: xt_lo[:, c, :]),
                                 (lambda c: w_lo[w][:, c, cols], lambda c: xt_hi[:, c, :])])
                if m == C - 1:
                    last.then_inc(filled, 1)

            def q_proj(b, p, m):
                if m == 0:
                    pe.wait_ge(xt_lo_done, PAIRS * b + p + 1)
                    if isinstance(b, int) and b == 0 and p < 3:
                        wait(pe, q_lo_done, p)
                qk(m, "q", q_filled, gc)

            def v_proj(b, p, j, bank=gc):
                n = PAIRS * b + p
                if j == 0 and bank is gc:
                    pe.wait_ge(q_lo_done, n + 1)
                elif j == 0:
                    wait(pe, v_done, n)
                rows = slice(P * j, P * (j + 1))
                last = products(bank[:, D * j:D * (j + 1)],
                                [(lambda c: xt_hi[:, c, rows], lambda c: w_hi["v"][:, c, :]),
                                 (lambda c: xt_hi[:, c, rows], lambda c: w_lo["v"][:, c, :]),
                                 (lambda c: xt_lo[:, c, rows], lambda c: w_hi["v"][:, c, :])])
                if j == 1:
                    last.then_inc(v_filled, 1)

            def k_proj(b, p, m, bank=gc):
                n = PAIRS * b + p
                if m == 0 and bank is gc:
                    pe.wait_ge(v_done, n + 1)
                elif m == 0:
                    wait(pe, k_lo_done, n)
                qk(m, "k", k_filled, bank)

            def max_scores(b, t, f, banks=(mx_bank,)):
                rg, heads = MX_FILLS[f]
                n = MXF * (TILES * b + t) + f
                if f == 0 and t % 2 == 0:
                    i, m = halves(t // 2)
                    pe.wait_ge(q_max_set[i], 32 * (PAIRS // 2 * b + m + 1))
                    pe.wait_ge(k_max_set[i], 32 * (PAIRS // 2 * b + m + 1))
                wait(pe, mx_done, n + 1 - len(banks))
                bank = banks[f % len(banks)]
                dst = bank[:, 0:WIN * len(heads)].rearrange("p (h k) -> p h k", k=WIN)
                hs = slice(0, len(heads))
                if t == 0:
                    mm(dst, ident16[:, :], window0[:, hs, :], start=True, stop=False, skip_group_check=True)
                else:
                    mm(dst[:, :, 0:QB], ident16[:, :], window[:, hs, 0:QB], start=True, stop=False, skip_group_check=True)
                    mm(dst[:, :, P:WIN], ident16[:, :], window[:, hs, P:WIN], start=False, stop=False, skip_group_check=True)
                for j, h in enumerate(heads):
                    for blk in range(P // QB):
                        at = P * t + QB * blk
                        last = mm(bank[QB * blk:QB * (blk + 1), WIN * j:WIN * (j + 1)],
                                  q_max[64 * rg:64 * rg + DK, h, at:at + QB],
                                  k_max[64 * rg:64 * rg + DK, h, at:at + WIN],
                                  start=False, stop=j == len(heads) - 1, skip_group_check=True)
                last.then_inc(mx_filled, 1)

            def turn_max(b, t):
                n = TILES * b + t
                pe.wait_ge(mx_done, MXF * (n + 1))
                wait(pe, ct_lo_done, n - 5)
                wait(pe, nm_done, n)
                nc.tensor.transpose(gb[0:H, 0:P], nmax[:, t % 2, :], ident[:, :]).then_inc(nm_filled, 1)

            def scores(b, t, f):
                n = TILES * b + t
                if f == 0:
                    for tt in ((0, 1) if t == 0 else (t + 1,) if t < TILES - 1 else ()):
                        i, m = halves(tt)
                        pe.wait_ge(nmax_stacked[i], 32 * (TILES // 2 * b + m + 1))
                        if tt % 2 == 0:
                            i, m = halves(tt // 2)
                            pe.wait_ge(q_stacked[i], 96 * (PAIRS // 2 * b + m + 1))
                            pe.wait_ge(k_stacked[i], 96 * (PAIRS // 2 * b + m + 1))
                wait(pe, exp_done, SC_FILLS * n + f - 1)
                q = 2 * P if t < TILES - 1 else P
                for j in range(2):
                    rg, h = divmod(2 * f + j, HB)
                    last = mm(sc_bank[f % 2][:, 2 * P * j:2 * P * j + q],
                              k_stack[64 * rg:64 * rg + SUMS, h, P * t:P * (t + 1)],
                              q_stack[64 * rg:64 * rg + SUMS, h, P * t:P * t + q], start=True, stop=True)
                last.then_inc(sc_filled, 1)

            def prob_v(b, t, f):
                n = TILES * b + t
                cg, nxt = divmod(f, 2)
                if nxt and t == TILES - 1:
                    return
                if f == 0:
                    pe.wait_ge(prob_masked, 2 * n + 1)
                    if t == 0:
                        wait(pe, u_done, n - 1)
                if f == 1:
                    wait(pe, u_done, n)
                if f == 4:
                    pe.wait_ge(prob_masked, 2 * n + 2)
                for j in range(4):
                    h = 4 * cg + j
                    last = mm(pv_bank[(t + nxt) % 2][32 * j:32 * (j + 1), P * cg:P * (cg + 1)],
                              v_ones[:, t, h, :], prob[:, t % 2, h, P * nxt:P * (nxt + 1)],
                              start=cg == 0 and (nxt == 1 or t == 0), stop=cg == 3 and not nxt, skip_group_check=True)
                if f == (7 if t < TILES - 1 else 6):
                    last.then_inc(pv_filled, 1)

            def turn_u(b, t):
                n = TILES * b + t
                pe.wait_ge(u_done, n + 1)
                wait(pe, x2_done, n)
                for cg in range(4):
                    last = nc.tensor.transpose(ga[:, P * cg:P * (cg + 1)], u[:, t % 2, P * cg:P * (cg + 1)], ident[:, :])
                last.then_inc(ut_filled, 1)

            def turn_c(b, t):
                n = TILES * b + t
                pe.wait_ge(cx_done, n + 1)
                wait(pe, t2_lo_done, n)
                if isinstance(n, int) and n == 0:
                    pe.wait_ge(nm_done, 6)
                flat = cx[:, :, :].rearrange("p h d -> p (h d)")
                for c in range(C):
                    last = nc.tensor.transpose(gb[:, P * c:P * (c + 1)], flat[:, P * c:P * (c + 1)], ident[:, :])
                last.then_inc(ct_filled, 1)

            def o_proj(dst, hi, lo):
                return products(dst, [(lambda c: hi[:, c, :], lambda c: w_hi["o"][:, c, :]),
                                      (lambda c: hi[:, c, :], lambda c: w_lo["o"][:, c, :]),
                                      (lambda c: lo[:, c, :], lambda c: w_hi["o"][:, c, :])])

            def turn_x2(b, t, later):
                n = TILES * b + t
                pe.wait_ge(xn2_done, n + 1)
                if later:
                    pe.wait_ge(nm_done, n + 7)
                else:
                    pe.wait_ge(ct_lo_done, n + 1)
                for c in range(C):
                    last = nc.tensor.transpose(gb[:, P * c:P * (c + 1)], xn2[:, P * c:P * (c + 1)], ident[:, :])
                last.then_inc(t2_filled, 1)

            def second_layer(b, t, later):
                n = TILES * b + t
                pe.wait_ge(t2_lo_done, n + 1)
                if later:
                    pe.wait_ge(cx_done, n + 2)
                else:
                    pe.wait_ge(x2_done, n + 1)
                products(ga[:, 0:D], [(lambda c: t2_hi[:, c, :], lambda c: w_sign[:, c, :]),
                                      (lambda c: t2_lo[:, c, :], lambda c: w_sign[:, c, :])]).then_inc(ff_filled, 1)

            def sum_bias(b):
                pe.wait_ge(vsum_step, TILES * (b + 1))
                pe.wait_ge(k_lo_done, PAIRS * (b + 1))
                for c in range(C):
                    last = mm(gc[:, P * c:P * (c + 1)], vsum[:, P * c:P * (c + 1)], ones[:, :], start=True, stop=True)
                last.then_inc(cb_filled, 1)

            def bias_proj(b):
                pe.wait_ge(cb_step, 3 * (b + 1))
                if isinstance(b, int) and b == 0:
                    pe.wait_ge(nm_done, 6)
                else:
                    pe.wait_ge(t2_lo_done, TILES * b)
                o_proj(gb[:, 0:D], cb_hi, cb_lo).then_inc(br_filled, 1)

            def out_proj(b, t):
                n = TILES * b + t
                pe.wait_ge(ct_lo_done, n + 1)
                wait(pe, y_done, n)
                o_proj(ga[:, 0:D], ct_hi, ct_lo).then_inc(op_filled, 1)

            def slot(b, t):
                now, part = parts(b, t)
                op, ff, tqv, k, mx, pv = (part[n] for n in ("op", "ff", "tqv", "k", "mx", "pv"))
                if now:
                    scores(b, t, 0)
                if op:
                    turn_u(*op)
                if part["nm"]:
                    turn_max(*part["nm"])
                if mx:
                    max_scores(*mx, 0)
                if tqv:
                    t1(*tqv)
                if pv:
                    prob_v(*pv, 0)
                if now:
                    scores(b, t, 1)
                if k:
                    k_proj(*k, 0)
                if mx:
                    max_scores(*mx, 1)
                if pv:
                    prob_v(*pv, 1)
                if now:
                    scores(b, t, 2)
                if ff:
                    turn_x2(*ff, part["nm"])
                if tqv:
                    q_proj(*tqv, 0)
                if mx:
                    max_scores(*mx, 2)
                if pv:
                    prob_v(*pv, 2)
                if now:
                    scores(b, t, 3)
                if now and t == 3:
                    bias_proj(b)
                if tqv:
                    q_proj(*tqv, 1)
                if k:
                    k_proj(*k, 1)
                if now and t == 3:
                    pe.wait_ge(brow_done, b + 1)
                if op:
                    turn_c(*op)
                if mx:
                    max_scores(*mx, 3)
                if pv:
                    prob_v(*pv, 3)
                if now:
                    scores(b, t, 4)
                if ff:
                    second_layer(*ff, op)
                if now:
                    scores(b, t, 5)
                if mx:
                    max_scores(*mx, 4)
                if pv:
                    prob_v(*pv, 4)
                    prob_v(*pv, 5)
                if tqv:
                    v_proj(*tqv, 0)
                if now and t == 2:
                    sum_bias(b)
                if now:
                    scores(b, t, 6)
                if op:
                    out_proj(*op)
                if mx:
                    max_scores(*mx, 5)
                if pv:
                    prob_v(*pv, 6)
                    prob_v(*pv, 7)
                if now:
                    scores(b, t, 7)
                if tqv:
                    v_proj(*tqv, 1)

            def both(proj, b, p, *bank):
                for m in range(2):
                    proj(b, p, m, *bank)

            pe.wait_ge(consts_done, 1)
            for p in range(2):
                t1(0, p, sc_bank[p])
            for p in range(2):
                if p == 0:
                    pe.wait_ge(w_lo_done, 1)
                both(q_proj, 0, p)
                if p == 0:
                    pe.wait_ge(w_lo_done, 2)
                both(v_proj, 0, p, ga)
                if p == 0:
                    pe.wait_ge(w_lo_done, 3)
                both(k_proj, 0, p, gb)
            t1(0, 2, sc_bank[0])
            pe.wait_ge(memset_done, 2)
            pe.wait_ge(windows_done, 1)
            for t in range(3):
                for f in range(MXF):
                    max_scores(0, t, f, (mx_bank, pv_bank[0]))
                if t == 0:
                    pe.wait_ge(k_lo_done, 2)
                if t < 2:
                    turn_max(0, t)
                if t == 1:
                    both(q_proj, 0, 2)
                    both(v_proj, 0, 2, ga)
            pe.wait_ge(q_lo_done, 3)
            pe.wait_ge(w_lo_done, 4)
            pe.wait_ge(w_sign_done, 2)
            pe.wait_ge(ones_stacked, 32)
            run(pe, slot)


def kernel(L0_attn_x, L0_attn_Wq, L0_attn_bq, L0_attn_Wk, L0_attn_bk, L0_attn_Wv, L0_attn_bv, L0_attn_Wo,
           L0_attn_bo, L0_ffn_weight):
    import numpy as np
    import concourse.bacc as bacc
    from concourse.bass_utils import run_bass_kernel_spmd

    def by_place(w):
        w = np.asarray(w)
        return w.reshape(C, HB, DK, -1).transpose(0, 2, 1, 3).reshape(D, -1)

    def columns(v):
        return np.ascontiguousarray(np.asarray(v).reshape(C, P).T)

    arrays = {
        "x": np.asarray(L0_attn_x),
        "wq_t": by_place(L0_attn_Wq).T,
        "wk_t": by_place(L0_attn_Wk).T,
        "wv_t": np.asarray(L0_attn_Wv).T,
        "wo_t": np.asarray(L0_attn_Wo).T,
        "wf_t": np.asarray(L0_ffn_weight).T,
        "bq_c": columns(by_place(L0_attn_bq)),
        "bk_c": columns(by_place(L0_attn_bk)),
        "bv_c": columns(L0_attn_bv),
        "bo_r": np.broadcast_to(np.asarray(L0_attn_bo), (P, D)),
    }
    arrays = {k: np.ascontiguousarray(v) for k, v in arrays.items()}
    nc = bacc.Bacc("TRN2", target_bir_lowering=False, num_devices=1)
    args = {k: nc.dram_tensor(k, v.shape, mybir.dt.from_np(v.dtype), kind="ExternalInput").ap() for k, v in arrays.items()}
    out = nc.dram_tensor("out", arrays["x"].shape, F32, kind="ExternalOutput").ap()
    build(nc, out=out, **args)
    result = run_bass_kernel_spmd(nc, [arrays], core_ids=[0])
    return result.results[0]["out"]
```
